# Optimizing a Trainium2 kernel written in Bass

```python
import numpy as np
import jax
import jax.numpy as jnp

def _softmax(x, axis=-1):
    return jax.nn.softmax(x, axis=axis)

def _gelu(x):
    return jax.nn.gelu(x, approximate=True)

def _silu(x):
    return jax.nn.silu(x)

def _sigmoid(x):
    return jax.nn.sigmoid(x)

def _layernorm(x, axis=-1, eps=1e-05):
    m = jnp.mean(x, axis=axis, keepdims=True)
    v = jnp.var(x, axis=axis, keepdims=True)
    return (x - m) / jnp.sqrt(v + eps)

def _scatter_add(tgt, idx, src, axis=0):
    return tgt.at[idx].add(src)

def _segment_sum(src, seg, n):
    return jax.ops.segment_sum(src, seg, n)
kernel_name = 'mk_adaln_d2_jaxref_r4_3f2461'

def setup_inputs(seed: int=0):
    np.random.seed(seed)
    _w = jnp.asarray

    def _L0_attn_setup():
        import jax, jax.numpy as jnp
        import numpy as np
        PI = float(np.pi)
        EPS = 1e-06
        key = jax.random.key(seed)
        k1, k2, k3, k4, k5 = jax.random.split(key, 5)
        B, T, D, H, Dh = (4, 1024, 256, 16, 64)

        def xavier(k, shape):
            fan_in, fan_out = (shape[-2], shape[-1])
            lim = float(np.sqrt(6.0 / (fan_in + fan_out)))
            return jax.random.uniform(k, shape, jnp.float32, -lim, lim)
        return {'query': jax.random.normal(k1, (B, T, D), jnp.float32), 'W_Q': xavier(k2, (H, D, 1)), 'W_K': xavier(k3, (H, D, 1)), 'W_V': xavier(k4, (H, D, Dh)), 'W_O': xavier(k5, (D, Dh, H))}
    _L0_attn_in = _L0_attn_setup()

    def _L0_ffn_setup():
        import jax, jax.numpy as jnp
        import numpy as np
        B, S, D, F, E, K = (4, 512, 256, 1024, 4, 2)
        key = jax.random.key(seed)
        k = jax.random.split(key, 6)
        x = jax.random.normal(k[0], (B, S, D), jnp.float32)
        router_w = jax.random.normal(k[1], (D, E), jnp.float32) * D ** (-0.5)
        router_b = jnp.zeros((E,), jnp.float32)
        w1 = jax.random.normal(k[2], (E, D, F), jnp.float32) * 0.02
        w3 = jax.random.normal(k[3], (E, D, F), jnp.float32) * 0.02
        w2 = jax.random.normal(k[4], (E, F, D), jnp.float32) * 0.02
        return {'x': x, 'router_w': router_w, 'router_b': router_b, 'w1': w1, 'w3': w3, 'w2': w2}
    _L0_ffn_in = _L0_ffn_setup()
    _L0_c = _w((lambda *s: np.random.randn(*s).astype(np.float32) * 0.05)(8, 256))
    _L0_wmod = _w((lambda *s: np.random.randn(*s).astype(np.float32) * 0.05)(256, 6 * 256) * 256 ** (-0.5))

    def _L1_attn_setup():
        import jax, jax.numpy as jnp
        import numpy as np
        H = 16
        G = 4
        DIM = 256
        HD = DIM // H // G
        key = jax.random.key(seed)
        k1, k2, k3 = jax.random.split(key, 3)
        x = jax.random.normal(k1, (8, 1024, DIM), dtype=jnp.float32)
        w_qkvw = jax.random.normal(k2, (DIM, 4 * DIM), dtype=jnp.float32) * 0.02
        w_out = jax.random.normal(k3, (DIM, DIM), dtype=jnp.float32) * 0.02
        return {'x': x, 'w_qkvw': w_qkvw, 'w_out': w_out}
    _L1_attn_in = _L1_attn_setup()

    def _L1_ffn_setup():
        import jax, jax.numpy as jnp
        import numpy as np
        B, S, H, FFN, E = (2, 512, 256, 1024, 8)
        key = jax.random.key(seed)
        k0, k1, k2, k3 = jax.random.split(key, 4)
        return {'hidden_states': jax.random.normal(k0, (B, S, H), dtype=jnp.float32), 'Wr': jax.random.normal(k1, (H, E), dtype=jnp.float32) * 0.02, 'br': jnp.zeros((E,), dtype=jnp.float32), 'W1': jax.random.normal(k2, (E, H, FFN), dtype=jnp.float32) * 0.02, 'W2': jax.random.normal(k3, (E, FFN, H), dtype=jnp.float32) * 0.02}
    _L1_ffn_in = _L1_ffn_setup()
    _L1_c = _w((lambda *s: np.random.randn(*s).astype(np.float32) * 0.05)(8, 256))
    _L1_wmod = _w((lambda *s: np.random.randn(*s).astype(np.float32) * 0.05)(256, 6 * 256) * 256 ** (-0.5))
    _d = {'L0_attn_query': _L0_attn_in['query'], 'L0_attn_W_Q': _L0_attn_in['W_Q'], 'L0_attn_W_K': _L0_attn_in['W_K'], 'L0_attn_W_V': _L0_attn_in['W_V'], 'L0_attn_W_O': _L0_attn_in['W_O'], 'L0_ffn_router_w': _L0_ffn_in['router_w'], 'L0_ffn_router_b': _L0_ffn_in['router_b'], 'L0_ffn_w1': _L0_ffn_in['w1'], 'L0_ffn_w3': _L0_ffn_in['w3'], 'L0_ffn_w2': _L0_ffn_in['w2'], 'L0_c': _L0_c, 'L0_wmod': _L0_wmod, 'L1_attn_w_qkvw': _L1_attn_in['w_qkvw'], 'L1_attn_w_out': _L1_attn_in['w_out'], 'L1_ffn_Wr': _L1_ffn_in['Wr'], 'L1_ffn_br': _L1_ffn_in['br'], 'L1_ffn_W1': _L1_ffn_in['W1'], 'L1_ffn_W2': _L1_ffn_in['W2'], 'L1_c': _L1_c, 'L1_wmod': _L1_wmod}
    _x0 = _d['L0_attn_query']
    _d['L0_attn_query'] = jax.random.normal(jax.random.fold_in(jax.random.key(seed), 1), (8, 512, 256), dtype=_x0.dtype)
    del _x0
    return _d

def reference(L0_attn_query, L0_attn_W_Q, L0_attn_W_K, L0_attn_W_V, L0_attn_W_O, L0_ffn_router_w, L0_ffn_router_b, L0_ffn_w1, L0_ffn_w3, L0_ffn_w2, L0_c, L0_wmod, L1_attn_w_qkvw, L1_attn_w_out, L1_ffn_Wr, L1_ffn_br, L1_ffn_W1, L1_ffn_W2, L1_c, L1_wmod):

    def _L0_attn_ref(query, W_Q, W_K, W_V, W_O):
        import jax, jax.numpy as jnp
        import numpy as np
        PI = float(np.pi)
        EPS = 1e-06
        q = jnp.einsum('btd,hdo->btho', query, W_Q)
        k = jnp.einsum('btd,hdo->btho', query, W_K)
        V = jnp.einsum('btd,hde->bthe', query, W_V)
        q = jnp.tanh(q) * (PI / 4)
        k = jnp.tanh(k) * (PI / 4)
        cos_k, sin_k = (jnp.cos(k), jnp.sin(k))
        cos_q, sin_q = (jnp.cos(q), jnp.sin(q))
        cos_KV = jnp.cumsum(cos_k * V, axis=1)
        sin_KV = jnp.cumsum(sin_k * V, axis=1)
        heads = cos_q * cos_KV + sin_q * sin_KV
        cos_K = jnp.cumsum(cos_k, axis=1)
        sin_K = jnp.cumsum(sin_k, axis=1)
        denom = cos_q * cos_K + sin_q * sin_K + EPS
        heads = heads / denom
        return jnp.einsum('deh,bthe->btd', W_O, heads)

    def _L0_ffn_ref(x, router_w, router_b, w1, w3, w2):
        import jax, jax.numpy as jnp
        import numpy as np
        B, S, D, F, E, K = (4, 512, 256, 1024, 4, 2)
        b, s, d = x.shape
        T = b * s
        e = router_w.shape[1]
        xf = x.reshape(T, d)
        logits = xf @ router_w + router_b
        probs = jax.nn.softmax(logits, axis=-1)
        top_p, top_i = jax.lax.top_k(probs, K)
        top_p = top_p / jnp.sum(top_p, axis=-1, keepdims=True)
        gates = jnp.zeros((T, e), xf.dtype).at[jnp.arange(T)[:, None], top_i].add(top_p)
        h = jax.nn.silu(jnp.einsum('td,edf->etf', xf, w1)) * jnp.einsum('td,edf->etf', xf, w3)
        expert_out = jnp.einsum('etf,efd->etd', h, w2)
        out = jnp.einsum('te,etd->td', gates, expert_out)
        return out.reshape(b, s, d)

    def _L1_attn_ref(x, w_qkvw, w_out):
        import jax, jax.numpy as jnp
        import numpy as np
        H = 16
        G = 4
        DIM = 256
        HD = DIM // H // G
        B, S, dim = x.shape
        qkvw = x @ w_qkvw
        chunks = jnp.split(qkvw, G, axis=-1)
        subs = [jnp.split(t, G, axis=-1) for t in chunks]
        q = jnp.concatenate([subs[i][0] for i in range(4)], axis=0)
        k = jnp.concatenate([subs[i][1] for i in range(4)], axis=0)
        v = jnp.concatenate([subs[i][2] for i in range(4)], axis=0)
        w = jnp.concatenate([subs[i][3] for i in range(4)], axis=0)

        def shp(t):
            return t.reshape(B * G, H, -1, HD).swapaxes(1, 2)
        q, k, v = (shp(q), shp(k), shp(v))
        w = w.reshape(B * G, H, -1, HD)
        scale = HD ** (-0.5)
        scores = q @ k.swapaxes(-2, -1) * scale
        attn = jax.nn.softmax(scores, axis=-1)
        o = (attn @ v).swapaxes(1, 2).reshape(B, S, dim)
        return o * w.reshape(B, S, dim) @ w_out

    def _L1_ffn_ref(hidden_states, Wr, br, W1, W2):
        import jax, jax.numpy as jnp
        import numpy as np
        B, S, H, FFN, E = (2, 512, 256, 1024, 8)
        b, s, h = hidden_states.shape
        x = hidden_states.reshape(-1, h)
        route = jax.nn.sigmoid(x @ Wr + br)
        max_prob = jnp.max(route, axis=1, keepdims=True)
        max_ind = jnp.argmax(route, axis=1)
        out = jnp.zeros_like(x)
        n_experts = Wr.shape[1]
        for e in range(n_experts):
            mask = (max_ind == e)[:, None].astype(x.dtype)
            y = jax.nn.gelu(x @ W1[e], approximate=False) @ W2[e]
            out = out + mask * y
        out = out * max_prob
        return out.reshape(b, s, h)
    x = L0_attn_query
    mod = (_silu(L0_c) @ L0_wmod).reshape(L0_c.shape[0], 6, 1, -1)
    sa, ca, ga, sb, cb, gb = (mod[:, 0], mod[:, 1], mod[:, 2], mod[:, 3], mod[:, 4], mod[:, 5])
    ga = (2 * (ga >= 0) - 1) * jnp.maximum(jnp.abs(ga), 0.25)
    gb = (2 * (gb >= 0) - 1) * jnp.maximum(jnp.abs(gb), 0.25)
    h = _layernorm(x, axis=-1) * (1 + ca) + sa
    x = x + ga * _L0_attn_ref(h, L0_attn_W_Q, L0_attn_W_K, L0_attn_W_V, L0_attn_W_O)
    h = _layernorm(x, axis=-1) * (1 + cb) + sb
    x = x + gb * _L0_ffn_ref(h, L0_ffn_router_w, L0_ffn_router_b, L0_ffn_w1, L0_ffn_w3, L0_ffn_w2)
    mod = (_silu(L1_c) @ L1_wmod).reshape(L1_c.shape[0], 6, 1, -1)
    sa, ca, ga, sb, cb, gb = (mod[:, 0], mod[:, 1], mod[:, 2], mod[:, 3], mod[:, 4], mod[:, 5])
    ga = (2 * (ga >= 0) - 1) * jnp.maximum(jnp.abs(ga), 0.25)
    gb = (2 * (gb >= 0) - 1) * jnp.maximum(jnp.abs(gb), 0.25)
    h = _layernorm(x, axis=-1) * (1 + ca) + sa
    x = x + ga * _L1_attn_ref(h, L1_attn_w_qkvw, L1_attn_w_out)
    h = _layernorm(x, axis=-1) * (1 + cb) + sb
    x = x + gb * _L1_ffn_ref(h, L1_ffn_Wr, L1_ffn_br, L1_ffn_W1, L1_ffn_W2)
    return x

_drawn_inputs = setup_inputs


def setup_inputs(seed=0):
    import zlib

    import numpy as np

    out = dict(_drawn_inputs(seed))
    spreads = {'L0_ffn_router_b': (0.0, 0.8), 'L1_ffn_br': (0.0, 0.8)}
    factors = {'L0_ffn_router_w': 8.0,
     'L0_ffn_w1': 8.0,
     'L0_ffn_w3': 8.0,
     'L0_ffn_w2': 8.0,
     'L1_attn_w_qkvw': 8.0,
     'L1_attn_w_out': 8.0,
     'L1_ffn_Wr': 3.664,
     'L1_ffn_W1': 3.486,
     'L1_ffn_W2': 3.4,
     'L1_c': 3.372,
     'L1_wmod': 3.383}
    for name, (base, spread) in spreads.items():
        noise = np.random.default_rng([zlib.crc32(name.encode()), seed]).standard_normal(out[name].shape)
        drawn = base * np.exp(spread * noise) if base else spread * noise
        out[name] = jnp.asarray(drawn.astype(out[name].dtype))
    for name, factor in factors.items():
        out[name] = (out[name] * factor).astype(out[name].dtype)
    return out
```

```python
import math

import concourse.bass as bass
from concourse import mybir

fp32 = mybir.dt.float32
i32 = mybir.dt.int32
f16 = mybir.dt.float16
ALU = mybir.AluOpType
ACT = mybir.ActivationFunctionType
AX = mybir.AxisListType

B, S, D = 8, 512, 256
T = B * S
NT = T // 128
PI = math.pi
BIGW = 38400


class Sem:

    def __init__(self, sem):
        self.sem, self.n = sem, 0

    def up(self, by):
        self.n += by
        return (self, self.n)


class Queue:

    def __init__(self, name):
        self.name, self.items, self.done, self.seen = name, [], None, {}

    def wait(self, *tokens):
        most = {}

        def collect(ts):
            for t in ts:
                if isinstance(t, list):
                    collect(t)
                elif t is not None:
                    most[t[0]] = max(most.get(t[0], 0), t[1])
        collect(tokens)
        for sem, n in most.items():
            if self.seen.get(sem, 0) < n:
                self.seen[sem] = n
                self.items.append(lambda e, s=sem.sem, n=n: e.wait_ge(s, n))

    def __call__(self, f, *after, mark=True):
        self.wait(*after)
        if not mark:
            self.items.append(f)
            return None
        t = self.done.up(1)
        self.items.append(lambda e, f=f, s=t[0].sem: f(e).then_inc(s, 1))
        return t

    def dma(self, sem, out, in_, *after):
        self.wait(*after)
        t = sem.up(16)
        self.items.append(lambda e: e.dma_start(out, in_).then_inc(sem.sem, 16))
        return t

    def scatter(self, sem, out, idx, in_, *after):
        self.wait(*after)
        t = sem.up(16)
        self.items.append(lambda e: e.indirect_dma_start(
            out, bass.IndirectOffsetOnAxis(idx, 0), in_, None).then_inc(sem.sem, 16))
        return t

    def gather(self, sem, out, in_, idx, *after):
        self.wait(*after)
        t = sem.up(16)
        self.items.append(lambda e: e.indirect_dma_start(
            out, None, in_, bass.IndirectOffsetOnAxis(idx, 0)).then_inc(sem.sem, 16))
        return t

    def play(self, e):
        for f in self.items:
            f(e)


class Ring:

    def __init__(self, bufs):
        self.bufs, self.free, self.i = bufs, [[] for _ in bufs], -1

    def next(self):
        self.i = (self.i + 1) % len(self.bufs)
        free, self.free[self.i] = self.free[self.i], []
        return self.bufs[self.i], free, self.free[self.i]


def program(nc, x_in, wqk_in, wv_in, wo_in, rw_in, rb_in, w1_in, w3_in, w2_in, c0_in, m0_in,
            qkvw_in, wout_in, wr_in, br_in, v1_in, v2_in, c1_in, m1_in, out, phases=4):
    from contextlib import ExitStack
    ctx = ExitStack()
    with ctx:
        def sb(name, shape, dt=fp32):
            return ctx.enter_context(nc.sbuf_tensor(name, shape, dt))

        def sem(name):
            return Sem(ctx.enter_context(nc.semaphore(name)))

        X = sb("X", [128, NT, D])
        BIG = sb("BIG", [128, BIGW])
        BIG16 = BIG[:, :].bitcast(f16)
        ident = sb("ident", [128, 128])
        ident16 = sb("ident16", [128, 128], f16)
        tri = sb("tri", [128, 128], f16)
        atri = sb("atri", [128, 128], f16)
        stri = sb("stri", [128, 128], f16)
        ones = sb("ones", [128, 128], f16)
        sel = sb("sel", [8, 8, 128])
        MOD = sb("MOD", [8, 2, 6 * D])
        modT = sb("modT", [128, 2, 4, 8])
        stat = sb("stat", [128, NT, 2])
        rstd = sb("rstd", [128, NT])
        half_pi = sb("half_pi", [128, 1])
        bnst = sb("bnst", [128, 4, 6])
        pcol = sb("pcol", [128, 1])
        iota_p = sb("iota_p", [128, 128])
        tile_no = sb("tile_no", [128, 2, NT])

        ps = [ctx.enter_context(nc.psum_tensor(f"ps{i}", [128, 512], fp32)) for i in range(8)]

        def dram(name, shape, dt=fp32):
            return nc.dram_tensor(name, shape, dt, kind="Internal").ap()

        def shaped(v, shape):
            if len(shape) == 1:
                return v
            names = "abcdef"[:len(shape)]
            return v.rearrange(f"p ({' '.join(names)}) -> p {' '.join(names)}",
                               **{k: s for k, s in zip(names[1:], shape[1:])})

        def view(off, *shape, dt=None, parts=128):
            n = math.prod(shape)
            words = n // 2 if dt == f16 else n
            assert off + words <= BIGW, (off, shape)
            v = BIG[0:parts, off:off + words]
            return shaped(v.bitcast(dt) if dt is not None else v, shape)

        class Area:

            def __init__(self, start):
                self.at = start

            def __call__(self, *shape, dt=None, parts=128):
                v = view(self.at, *shape, dt=dt, parts=parts)
                n = math.prod(shape)
                self.at += (n + 1) // 2 if dt == f16 else n
                return v

            def ring(self, n, *shape, dt=None):
                return Ring([self(*shape, dt=dt) for _ in range(n)])

            def pair(self, *shape):
                return self(*shape, dt=f16), self(*shape, dt=f16)

            def pairs(self, n, *shape):
                return Ring([self.pair(*shape) for _ in range(n)])

        pe, dve, act, pool, sp = (Queue(n) for n in ("pe", "dve", "act", "pool", "sp"))

        def phase_sems(n):
            for q in (pe, dve, act, pool):
                q.done = sem(f"{q.name}_{n}")

        def now(*queues):
            return [(q.done, q.done.n) for q in (queues or (pe, dve, act, pool)) if q.done.n]

        def mm(out, lhsT, rhs, start, stop, *after, mark=False):
            return pe(lambda e: e.matmul(out, lhsT, rhs, start=start, stop=stop, skip_group_check=True),
                      *after, mark=mark)

        def mm3(out, lhs, rhs, start, stop, *after, mark=False):
            mm(out, lhs[0], rhs[0], start, False, *after)
            mm(out, lhs[0], rhs[1], False, False)
            return mm(out, lhs[1], rhs[0], False, stop, mark=mark)

        def tp(out, in_, *after, mark=False, n=128):
            return pe(lambda e: e.transpose(out, in_, ident[0:n, 0:n]), *after, mark=mark)

        def tp16(out, in_, *after, mark=False):
            return pe(lambda e: e.transpose(out, in_, ident16[:, :]), *after, mark=mark)

        def copy(q, out, in_, *after):
            if q is act:
                return act(lambda e: e.activation(out, in_, ACT.Copy), *after)
            return q(lambda e: e.tensor_copy(out, in_), *after)

        def tt(q, out, a, b, op, *after):
            return q(lambda e: e.tensor_tensor(out, a, b, op), *after)

        def split(pair, src, q_lo, *after):
            h = copy(act, pair[0], src, *after)
            return [h, tt(q_lo, pair[1], src, pair[0], ALU.subtract, h)]

        def bank(i, *shape, dt=None):
            n = math.prod(shape)
            if dt == f16:
                return shaped(ps[i][:, 0:n // 2].bitcast(f16), shape)
            return shaped(ps[i][:, 0:n], shape)

        def bc(ap, axis, n):
            a = ap.unsqueeze(axis)
            shape = list(a.shape)
            shape[axis] = n
            return a.broadcast_to(shape)

        phase_sems(0)

        l_x = [sem(f"l_x{i}") for i in range(4)]
        xt = []
        xv = x_in.rearrange("(t p) d -> p t d", p=128)
        l_c = sem("l_c")
        area = Area(22912)
        WM = area(2, 2, 6 * D)
        CS = area(2, D, parts=8)
        cT = area(2, 2, 8)
        GT = area(2, 2, D, parts=8)
        mod_end = area.at
        sp.dma(l_c, CS[:, 0, :], c0_in)
        sp.dma(l_c, CS[:, 1, :], c1_in)
        for i in range(4):
            xt.append(sp.dma(l_x[i], X[:, 8 * i:8 * i + 8, :], xv[:, 8 * i:8 * i + 8, :]))
            if i == 0:
                sp.dma(l_c, WM[:, 0], m0_in.rearrange("(k p) n -> p k n", p=128))
                t_c = sp.dma(l_c, WM[:, 1], m1_in.rearrange("(k p) n -> p k n", p=128))

        t = [pool(lambda e, a=a, v=v: e.memset(a, v)) for a, v in
             ((ident[:, :], 0.0), (tri[:, :], 1.0), (stri[:, :], 1.0), (atri[:, :], 1.0),
              (ones[:, :], 1.0), (sel[:, :, :], 0.0), (half_pi[:, :], PI / 2))]

        def affine(ap, cmp, fill, base, pattern, cm, *after):
            return pool(lambda e: e.affine_select(out=ap, in_=ap, compare_op=cmp, fill=fill, base=base,
                                                  pattern=pattern, channel_multiplier=cm), *after)

        def iota(ap, pattern, base=0, cm=0, *after):
            return pool(lambda e: e.iota(ap, pattern, base=base, channel_multiplier=cm,
                                         allow_small_or_imprecise_dtypes=True), *after)
        t_id = affine(ident[:, :], ALU.not_equal, 1.0, 0, [[-1, 128]], 1, t[0])
        t_tri = affine(tri[:, :], ALU.is_ge, 0.0, 0, [[1, 128]], -1, t[1])
        t_stri = affine(stri[:, :], ALU.is_ge, 0.0, -1, [[1, 128]], -1, t[2])
        t_atri = affine(atri[:, :], ALU.is_ge, 0.0, -1, [[-1, 128]], 1, t[3])
        t_sel = affine(sel[:, :, :], ALU.not_equal, 1.0, 0, [[-1, 8], [0, 128]], 1, t[5])
        t_id16 = copy(pool, ident16[:, :], ident[:, :], t_id)
        iota(pcol[:, :], [[0, 1]], 0, 1)
        iota(iota_p[:, :], [[1, 128]])
        t_iota = iota(tile_no[:, :, :], [[NT, 2], [1, NT]], 1)
        t_ones, t_hp = t[4], t[6]

        t_silu = act(lambda e: e.activation(CS, CS, ACT.Silu), t_c)
        pT = bank(0, 2, 2, 8)
        for l in range(2):
            for k in range(2):
                t_tp = tp(pT[:, l, k, :], CS[:, l, k * 128:(k + 1) * 128], t_silu, t_id, mark=True, n=8)
        t_cT = copy(dve, cT, pT, t_tp)
        t_prev = None
        modt = []
        for l in range(2):
            for j in range(3):
                for k in range(2):
                    t_m = mm(ps[1 + j][0:8, :], cT[:, l, k, :], WM[:, l, k, 512 * j:512 * j + 512],
                             k == 0, k == 1, t_cT, t_prev, mark=(k == 1))
            for j in range(3):
                t_prev = copy(dve, MOD[:, l, 512 * j:512 * j + 512], ps[1 + j][0:8, :], t_m)
            pc = bank(4 + l, 4, 8)
            for blk in range(4):
                for k in range(2):
                    t_m = mm(pc[:, blk, :], WM[:, l, k, 128 * blk:128 * blk + 128], cT[:, l, k, :],
                             k == 0, k == 1, mark=(k == 1))
            t_mt = copy(dve, modT[:, l, :, :], pc, t_m)
            t_mt = dve(lambda e, l=l: e.tensor_scalar(modT[:, l, 2:4, :], modT[:, l, 2:4, :], 1.0, None, ALU.add), t_mt)
            modt.append(t_mt)
        gview = MOD.rearrange("b l (u v d) -> b l u v d", u=2, v=3)[:, :, :, 2, :]
        cview = MOD.rearrange("b l (u v d) -> b l u v d", u=2, v=3)[:, :, :, 1, :]
        for l in range(2):
            g = gview[:, l]
            t1 = dve(lambda e, g=g, l=l: e.tensor_scalar(GT[:, l], g, -1.0, None, ALU.mult), t_prev)
            t1 = tt(dve, GT[:, l], GT[:, l], g, ALU.max, t1)
            t1 = dve(lambda e, g=g, l=l: e.tensor_scalar(GT[:, l], GT[:, l], 0.25, None, ALU.max), t1)
            t2 = dve(lambda e, g=g: e.tensor_scalar(g, g, 0.0, 2.0, ALU.is_ge, ALU.mult), t1)
            t2 = dve(lambda e, g=g, l=l: e.scalar_tensor_tensor(out=g, in0=g, scalar=-1.0, in1=GT[:, l],
                                                                op0=ALU.add, op1=ALU.mult), t2)
            t_mod = dve(lambda e, l=l: e.tensor_scalar(cview[:, l], cview[:, l], 1.0, None, ALU.add), t2)
        t_mod_done = now(pe, dve, act)

        bn_last = [None] * 4

        def tile_stats(i, *ready):
            r = i % 4
            a = dve(lambda e: e.bn_stats(bnst[:, r, :], X[:, i, :]), bn_last[r], *ready)
            bn_last[r] = dve(lambda e: e.bn_aggr(stat[:, i, :], bnst[:, r, :]), a)
            return bn_last[r]

        def rstd_of(i, j, *ready):
            a = dve(lambda e: e.tensor_scalar(rstd[:, i:j], stat[:, i:j, 1], 1e-5, None, ALU.add), *ready)
            a = act(lambda e: e.activation(rstd[:, i:j], rstd[:, i:j], ACT.Sqrt), a)
            return dve(lambda e: e.reciprocal(rstd[:, i:j], rstd[:, i:j]), a)

        def xnorm(dst, i, *after):
            return dve(lambda e: e.tensor_scalar(dst, X[:, i, :], stat[:, i, 0:1], rstd[:, i:i + 1],
                                                 ALU.subtract, ALU.mult), *after)

        def norm_T(l, place, rings, banks, t_stats, tiles):
            ends = []
            xn_ring, v_ring = rings
            for n, i in enumerate(tiles):
                xn, free, users = xn_ring.next()
                a = xnorm(xn, i, t_stats(i), free)
                bk, bfree, busers = banks.next()
                for k in range(2):
                    a = tp(bk[:, k * 128:(k + 1) * 128], xn[:, k * 128:(k + 1) * 128], a, bfree, mark=True)
                users.append(a)
                v, vfree, vusers = v_ring.next()
                for k in range(2):
                    m = act(lambda e, k=k, i=i, v=v, bk=bk: e.activation(
                        v[:, k, :], bk[:, k * 128:(k + 1) * 128], ACT.Identity,
                        bias=modT[:, l, k, i // 4:i // 4 + 1], scale=modT[:, l, 2 + k, i // 4:i // 4 + 1]),
                        a, modt[l], vfree)
                    busers.append(m)
                hi, lo, src = place(n, v)
                m = copy(act, hi, src, m)
                m = tt(pool, lo, src, hi, ALU.subtract, m)
                vusers.append(m)
                ends.append(m)
            return ends

        def gates(l, which, bk, b, *after):
            return mm(bk[:, 0:256], sel[0:8, b, :], MOD[0:8, l, (2 + 3 * which) * D:(3 + 3 * which) * D],
                      True, True, t_mod, t_sel, *after, mark=True)

        def slab_list(l):
            E, ins = ((4, ((w1_in, 2), (w3_in, 2), (w2_in, 8))), (8, ((v1_in, 2), (v2_in, 8))))[l]
            return [(x, n, w[x].rearrange("(k p) n -> p k n", p=128), k) for x in range(E) for n, (w, k) in enumerate(ins)]

        WD = [dram("WD0", [128, 4 * 3 * 4096], f16), dram("WD1", [128, 8 * 2 * 4096], f16)]
        st_sem = [sem(f"l_st{i}") for i in range(2)]
        sv_sem = [sem(f"l_sv{i}") for i in range(2)]
        conv_n = [0]

        def convert(l, piece, stage, halves, q_lo):
            x, n, src, k = slab_list(l)[piece]
            nslab = (3, 2)[l]
            for hf in range(2):
                st, free, users = stage.next()
                i = conv_n[0] % 2
                conv_n[0] += 1
                a = sp.dma(st_sem[i], shaped(st, (k // 2, 2048 // k)), src[:, hf * k // 2:(hf + 1) * k // 2, :], free)
                pr, pfree, pusers = halves.next()
                s_ = split(pr, st, q_lo, a, pfree)
                users.extend(s_)
                for m in range(2):
                    at = (x * 2 * nslab + m * nslab + n) * 2048 + hf * 1024
                    pusers.append(sp.dma(sv_sem[i], WD[l][:, at:at + 1024], pr[m], s_))

        area = Area(0)
        hTh, hTl = area.pair(2, T)
        QC = area(NT, 32)
        QS = area(NT, 32)
        TH = area(NT, 32)
        DN = TH[:, 0:16, :].rearrange("p a b -> p (a b)").rearrange("p (t n) -> p t n", n=16)
        D2 = TH[:, 16:32, :].rearrange("p a b -> p (a b)").rearrange("p (t n) -> p t n", n=16)
        Wqk, Wv, Wo = area.pair(2, 32), area.pair(2, 1024), area.pair(8, D)
        stage = area.ring(2, 1024)
        halves = area.pairs(2, 1024)
        xnr, vr0 = area.ring(3, D), area.ring(2, 2, 128)
        GB = area(8, D)
        lap = area.at
        assert lap <= 22912, lap
        wst = view(mod_end, 4160)
        l_w = sem("l_w")
        t_lw = sp.dma(l_w, shaped(wst[:, 0:64], (2, 32)), wqk_in.rearrange("(k p) n -> p k n", p=128))
        t_lw = sp.dma(l_w, shaped(wst[:, 64:2112], (2, 1024)), wv_in.rearrange("(k p) n -> p k n", p=128))
        t_lw = sp.dma(l_w, shaped(wst[:, 2112:4160], (8, 256)), wo_in.rearrange("(k p) n -> p k n", p=128))
        ts = []
        for q4 in range(4):
            for i in range(8 * q4, 8 * q4 + 8):
                a = tile_stats(i, xt[i // 8])
            ts.append(rstd_of(8 * q4, 8 * q4 + 8, a))
        t_w = split([w.rearrange("p a b -> p (a b)") for w in Wqk], wst[:, 0:64], dve, t_lw)
        t_w += split([w.rearrange("p a b -> p (a b)") for w in Wv], wst[:, 64:2112], dve, t_lw)
        t_w += split([w.rearrange("p a b -> p (a b)") for w in Wo], wst[:, 2112:4160], dve, t_lw)
        tr = Ring([ps[6], ps[7]])
        t_hT = norm_T(0, lambda n, v: (hTh[:, :, n * 128:(n + 1) * 128], hTl[:, :, n * 128:(n + 1) * 128], v),
                      (xnr, vr0), tr, lambda i: ts[i // 8], range(NT))
        qkp = [bank(i, 16, 32) for i in range(2)]

        def hT_of(i, k):
            return hTh[:, k, i * 128:(i + 1) * 128], hTl[:, k, i * 128:(i + 1) * 128]

        for i in range(NT):
            for k in range(2):
                t_qk = mm3(qkp[i // 16][:, i % 16, :], hT_of(i, k), (Wqk[0][:, k, :], Wqk[1][:, k, :]),
                           k == 0, k == 1, t_hT[i], t_w, t_cT, mark=(k == 1))
        t_th = [act(lambda e, j=j: e.activation(TH[:, 16 * j:16 * j + 16, :], qkp[j], ACT.Tanh), t_qk) for j in range(2)]
        t_qc = act(lambda e: e.activation(QC, TH, ACT.Sin, bias=half_pi[:, 0:1], scale=PI / 4), t_th, t_hp)
        t_qs = act(lambda e: e.activation(QS, TH, ACT.Sin, scale=PI / 4), t_th)
        area = Area(lap)
        KVF = area.ring(2, 2, 1024)
        KVP = area.pairs(2, 2, 1024)
        TM = area.ring(1, 2, 1024)
        HD = area.ring(2, 1024)
        HT = area.pairs(1, 8, 128)
        YG = area.ring(2, D)
        cks = area(2, 2, NT, 16, dt=f16)
        area_b = area.at
        for j, src, tq in ((0, QC, t_qc), (1, QS, t_qs)):
            tk = split((cks[:, 0, j], cks[:, 1, j]), src[:, :, 16:32], dve, tq, t_mod_done, t_w)
            o = bank(2 + j, 8, 4, 16)
            for m in range(2):
                s4 = cks[:, m, j].rearrange("p (b c) n -> p b c n", c=4)
                mm(o, tri[:, :], s4, m == 0, False, tk, t_tri, t_ones)
                for back in range(1, 4):
                    for b in range(8):
                        end = m == 1 and back == 3 and b == 7
                        t_cum = mm(o[:, b, back:4, :], ones[:, :], s4[:, b, 0:4 - back, :], False, end, mark=end)
        cumc = bank(2, NT, 16)
        cums = bank(3, NT, 16)
        a = tt(dve, DN, QC[:, :, 0:16], cumc, ALU.mult, t_cum)
        b_ = tt(dve, D2, QS[:, :, 0:16], cums, ALU.mult, t_cum)
        a = dve(lambda e: e.scalar_tensor_tensor(out=DN, in0=DN, scalar=1e-6, in1=D2, op0=ALU.add, op1=ALU.add), a, b_)
        a = dve(lambda e: e.reciprocal(DN, DN), a)
        b_ = tt(dve, QC[:, :, 0:16], QC[:, :, 0:16], DN, ALU.mult, a)
        t_q = tt(dve, QS[:, :, 0:16], QS[:, :, 0:16], DN, ALU.mult, a)

        t_gb = None
        for b in range(8):
            g = gates(0, 0, ps[4], b, t_mod_done, t_gb)
            t_gb = copy(dve, GB[:, b, :], ps[4][:, 0:256], g)
        vr = Ring([ps[4], ps[5]])
        vr.free = [[t_gb], []]
        tr2 = tr
        acc_free = [t_q, b_]
        t_kv0 = now(pe, dve, act)

        def heads_of(ap, n=8):
            return ap.rearrange("p (h e) -> p h e", e=64)

        def l0_values(i):
            kvf, free, users = KVF.next()
            kvp, pfree, pusers = KVP.next()
            ends = []
            for hf in range(2):
                bk, bfree, busers = vr.next()
                for k in range(2):
                    a = mm3(bk[:, :], hT_of(i, k), [w[:, k, hf * 512:hf * 512 + 512] for w in Wv],
                            k == 0, k == 1, bfree, mark=(k == 1))
                for j, q in ((0, QC), (1, QS)):
                    cut = slice(hf * 512, hf * 512 + 512)
                    f = tt(dve, heads_of(kvf[:, j, cut]), heads_of(bk[:, :]),
                           bc(q[:, i, 16 + 8 * hf:24 + 8 * hf], 2, 64), ALU.mult, a, free, t_kv0)
                    busers.append(f)
                    s_ = split((kvp[0][:, j, cut], kvp[1][:, j, cut]), kvf[:, j, cut], pool, f, pfree)
                    users.extend(s_)
                    ends.extend(s_)
            return kvp, ends, pusers

        def l0_out(i, hd, t_hd, hd_users):
            ht, hfree, husers = HT.next()
            cp = []
            for q in range(2):
                bk, bfree, busers = tr2.next()
                for j in range(4):
                    a = tp(bk[:, j * 128:(j + 1) * 128], hd[:, (4 * q + j) * 128:(4 * q + j + 1) * 128], t_hd, bfree,
                           mark=(j == 3))
                hd_users.append(a)
                s_ = split([h[:, 4 * q:4 * q + 4, :] for h in ht], bk[:, :].rearrange("p (j n) -> p j n", j=4), dve, a, hfree)
                busers.extend(s_)
                cp.append(s_)
            return ht, cp, husers

        def l0_proj(i, ht, cp, husers):
            bk, bfree, busers = vr.next()
            for j in range(8):
                m = mm3(bk[:, 0:256], [h[:, j, :] for h in ht], [w[:, j, :] for w in Wo],
                        j == 0, j == 7, cp[j // 4], bfree, mark=(j == 7))
            husers.append(m)
            yg, yfree, yusers = YG.next()
            y = tt(dve, yg, bk[:, 0:256], GB[:, i // 4, :], ALU.mult, m, yfree)
            busers.append(y)
            y = tt(dve, X[:, i, :], X[:, i, :], yg, ALU.add, y)
            yusers.append(y)
            return y

        t_x = [None] * NT
        late = None
        n_conv = len(slab_list(0))
        vals = l0_values(0)
        for i in range(NT):
            kv, ends, kusers = vals
            first = i % 4 == 0
            for j in range(2):
                for hf in range(2):
                    for m2 in range(2):
                        end = j == 1 and hf == 1 and m2 == 1
                        m = mm(ps[2 * j + hf][:, :], tri[:, :], kv[m2][:, j, hf * 512:hf * 512 + 512],
                               first and m2 == 0, False, ends, acc_free, mark=end)
            tm, tfree, tusers = TM.next()
            reads = []
            for j, q in ((0, QC), (1, QS)):
                for hf in range(2):
                    reads.append(tt(dve, heads_of(tm[:, j, hf * 512:hf * 512 + 512]), heads_of(ps[2 * j + hf][:, :]),
                                    bc(q[:, i, 8 * hf:8 * hf + 8], 2, 64), ALU.mult, m, tfree))
            if late is not None:
                got = l0_out(*late)
            if i + 1 < NT:
                vals = l0_values(i + 1)
            acc_free = reads
            if i % 4 != 3:
                for j in range(2):
                    for hf in range(2):
                        for m2 in range(2):
                            end = j == 1 and hf == 1 and m2 == 1
                            m = mm(ps[2 * j + hf][:, :], atri[:, :], kv[m2][:, j, hf * 512:hf * 512 + 512], False, True,
                                   reads, t_atri, mark=end)
            kusers.append(m)
            hd, hfree, husers = HD.next()
            t_hd = tt(dve, hd, tm[:, 0], tm[:, 1], ALU.add, reads, hfree)
            tusers.append(t_hd)
            if late is not None:
                t_x[late[0]] = l0_proj(late[0], *got)
            late = (i, hd, t_hd, husers)
            if i >= 2 and (i - 2) % 2 == 0 and (i - 2) // 2 < n_conv:
                convert(0, (i - 2) // 2, stage, halves, pool)
        got = l0_out(*late)
        t_x[late[0]] = l0_proj(late[0], *got)
        t_conv = [[(s_, s_.n) for s_ in sv_sem]]

        def moe(l, E, CH, w_rt, b_rt, gated, ready, t_x, t_wd):
            NS = CH * NT + E - 1
            nslab = 3 if gated else 2
            span = 2 * nslab * 2048
            HB = dram(f"HB{l}", [T, 2 * D], f16)
            YT = dram(f"YT{l}", [(CH * NT + NS) * 128, D])
            area = Area(E * span // 2)
            SL = [area(NT) for c in range(CH)]
            GV = [area(NT) for c in range(CH)]
            ei = area(NS).bitcast(i32)
            gi = area(NS).bitcast(i32)
            yi = area(NS).bitcast(i32)
            base = area.at
            l_r = sem(f"l_r{l}")
            RWf = area(2, E)
            RW = area.pair(2, E)
            RB = area(E)
            sp.dma(l_r, RWf, w_rt.rearrange("(k p) n -> p k n", p=128), ready)
            t_r = sp.dma(l_r, RB, b_rt.unsqueeze(0).broadcast_to([128, E]), ready)
            t_rw = split([w.rearrange("p a b -> p (a b)") for w in RW], RWf.rearrange("p a b -> p (a b)"), dve, t_r, ready)
            LG = area(NT, E)
            HR = area.ring(2, D)
            HP = area.ring(3, 2, D, dt=f16)
            HTR = area.ring(2, 4, 128, dt=f16)
            HBv = HB.rearrange("(t p) d -> p t d", p=128)
            everything = now()
            trb = Ring([ps[6], ps[7]])
            trb.free = [list(everything) for _ in range(2)]
            scb = Ring([ps[4], ps[5]])
            scb.free = [list(everything) for _ in range(2)]
            lgp = bank(0, NT, E)
            l_hb = [sem(f"l_hb{l}_{i}") for i in range(3)]
            l_ew = sem(f"l_ew{l}")
            for x in range(E):
                t_w = sp.dma(l_ew, BIG16[:, x * span:(x + 1) * span], WD[l][:, x * span:(x + 1) * span], ready, t_wd)
            st4 = []
            for g4 in range(0, NT, 8):
                for i in range(g4, g4 + 8):
                    a = tile_stats(i, t_x[i])
                st4.append(rstd_of(g4, g4 + 8, a))

            def rows_T(src, *after):
                bk, bfree, busers = trb.next()
                b16 = shaped(bk[:, 0:256].bitcast(f16), (4, 128))
                for k in range(4):
                    m = tp16(b16[:, k, :], src[:, k * 128:(k + 1) * 128], *after, bfree, mark=(k == 3))
                return b16, m, busers

            for i in range(NT):
                b = i // 4
                if i % 4 == 0:
                    sc, sfree, susers = scb.next()
                    t_sc = mm(sc[:, :], sel[0:8, b, :], MOD[0:8, l, 3 * D:5 * D], True, True, t_mod, t_sel, sfree, mark=True)
                h, hfree, husers = HR.next()
                a = xnorm(h, i, st4[i // 8], hfree, ready)
                a = tt(dve, h, h, sc[:, 256:512], ALU.mult, a, t_sc)
                a = tt(dve, h, h, sc[:, 0:256], ALU.add, a)
                if i % 4 == 3:
                    susers.append(a)
                hp, pfree, pusers = HP.next()
                s_ = split((hp[:, 0, :], hp[:, 1, :]), h, pool, a, pfree)
                husers.extend(s_)
                flat = hp.rearrange("p a b -> p (a b)")
                pusers.append(sp.dma(l_hb[i % 3], HBv[:, i, :], flat, s_))
                b16, m, busers = rows_T(flat, s_)
                pusers.append(m)
                ht, tfree, tusers = HTR.next()
                a = copy(act, ht, b16, m, tfree)
                busers.append(a)
                for k in range(2):
                    m = mm3(lgp[:, i, :], (ht[:, k, :], ht[:, 2 + k, :]), [w[:, k, :] for w in RW], k == 0, k == 1,
                            a, t_rw, everything, mark=(k == 1))
                tusers.append(m)
            t_hb = [(s_, s_.n) for s_ in l_hb]
            cur = tt(dve, LG, lgp, bc(RB, 1, NT), ALU.add, m, t_r)
            late_words = area.at
            MX, W3, PR = area(NT), area(NT, E), area(NT, E)
            AL = area(NT, E, dt=f16)
            OH = [area(NT, E) for _ in range(CH)]
            dec = area(E)
            t_io = iota(dec, [[-1, E]], E, 0, ready)
            if CH == 2:
                cur = dve(lambda e: e.tensor_reduce(MX, LG, AX.X, ALU.max), cur)
                cur = tt(dve, PR, LG, bc(MX, 2, E), ALU.subtract, cur)
                cur = act(lambda e: e.activation(PR, PR, ACT.Exp), cur)
                cur = dve(lambda e: e.tensor_reduce(MX, PR, AX.X, ALU.add), cur)
                cur = dve(lambda e: e.reciprocal(MX, MX), cur)
                cur = tt(dve, PR, PR, bc(MX, 2, E), ALU.mult, cur)
            else:
                cur = act(lambda e: e.activation(PR, LG, ACT.Sigmoid), cur)
            for c in range(CH):
                cur = dve(lambda e, c=c: e.tensor_reduce(GV[c], PR, AX.X, ALU.max), cur)
                cur = tt(dve, W3, PR, bc(GV[c], 2, E), ALU.is_ge, cur)
                cur = tt(dve, W3, W3, bc(dec, 1, NT), ALU.mult, cur, t_io)
                cur = dve(lambda e: e.tensor_reduce(MX, W3, AX.X, ALU.max), cur)
                cur = tt(dve, OH[c], W3, bc(MX, 2, E), ALU.is_equal, cur)
                if c + 1 < CH:
                    cur = dve(lambda e, c=c: e.scalar_tensor_tensor(out=PR, in0=OH[c], scalar=-2.0, in1=PR,
                                                                    op0=ALU.mult, op1=ALU.add), cur)
            if CH == 2:
                cur = tt(dve, MX, GV[0], GV[1], ALU.add, cur)
                cur = dve(lambda e: e.reciprocal(MX, MX), cur)
                for c in range(2):
                    cur = tt(dve, GV[c], GV[c], MX, ALU.mult, cur)
                cur = tt(dve, AL, OH[0], OH[1], ALU.add, cur)
            else:
                cur = copy(dve, AL, OH[0], cur)
            rk, ct = bank(1, NT, E), bank(2, NT, E)
            mm(rk, stri[:, :], AL, True, True, cur, t_stri, t_ones)
            m = mm(ct, ones[:, :], AL, True, True, mark=True)
            CI, zz, cs = area(E, NT), area(NT), area(E, NT)
            cur = dve(lambda e: e.memset(zz, 0.0), m)
            cur = copy(dve, cs, ct.rearrange("p t e -> p e t"), cur)
            for x in range(E):
                t_last = dve(lambda e, x=x: e.tensor_tensor_scan(out=CI[:, x, :], data0=cs[:, x, :], data1=zz, initial=0.0,
                                                                 op0=ALU.add, op1=ALU.add), cur)
            n_i = area(E).bitcast(i32)
            n_p, ends_, bases = area(E), area(E), area(E)
            cur = dve(lambda e: e.tensor_scalar(n_p, CI[:, :, NT - 1], 127.0, None, ALU.add), t_last)
            cur = copy(dve, n_i, n_p, cur)
            cur = dve(lambda e: e.tensor_scalar(n_i, n_i, 7, 7, ALU.arith_shift_right, ALU.arith_shift_left), cur)
            cur = copy(dve, n_p, n_i, cur)
            cur = dve(lambda e: e.tensor_tensor_scan(out=ends_, data0=n_p, data1=zz[:, 0:E], initial=0.0,
                                                     op0=ALU.add, op1=ALU.add), cur)
            cur = tt(dve, bases, ends_, n_p, ALU.subtract, cur)
            cur = tt(dve, CI, CI, cs, ALU.subtract, cur)
            cur = tt(dve, CI, CI, bc(bases, 2, NT), ALU.add, cur)
            PS_ = area(NT, E)
            cur = tt(dve, PS_, rk, CI.rearrange("p e t -> p t e"), ALU.add, cur)
            for c in range(CH):
                cur = tt(dve, W3, PS_, OH[c], ALU.mult, cur)
                cur = dve(lambda e, c=c: e.tensor_reduce(SL[c], W3, AX.X, ALU.add), cur)
            it = area(NS)
            ex = area(NS)
            it128 = area(NS)
            t_it = iota(it, [[1, NS]], 0, 0, ready)
            t_it = iota(it128, [[128, NS]], 0, 0, ready)
            lap = Area(base) if l else area
            if l:
                dve.wait(now(pe, act, pool), t_hb)
            cmp_ = lap(NS, E)
            cur = tt(dve, cmp_, bc(ends_, 1, NS), bc(it128, 2, E), ALU.is_le, cur, t_it)
            cur = dve(lambda e: e.tensor_reduce(ex, cmp_, AX.X, ALU.add), cur)
            cur = dve(lambda e: e.tensor_scalar(ex, ex, float(E - 1), float(span), ALU.min, ALU.mult), cur)
            t_ei = copy(dve, ei, ex, cur)
            s_i, s_lo, s_hi = area(NT).bitcast(i32), area(NT), area(NT)
            s_j = area(NT).bitcast(i32)
            G = 8
            S1 = lap.ring(2, G, 128, dt=f16)
            A1 = lap.ring(2, G, 2, NS, dt=f16)
            assert not l or lap.at <= late_words
            mp = bank(3, 2, NS)
            cur = t_ei
            for c in range(CH):
                cur = copy(dve, s_i, SL[c], cur)
                cur = dve(lambda e: e.tensor_scalar(s_j, s_i, 7, None, ALU.arith_shift_right), cur)
                cur = copy(dve, s_hi, s_j, cur)
                cur = dve(lambda e, c=c: e.scalar_tensor_tensor(out=s_lo, in0=s_hi, scalar=-128.0, in1=SL[c],
                                                                op0=ALU.mult, op1=ALU.add), cur)
                for g in range(0, NT, G):
                    s1, sfree, susers = S1.next()
                    a1, afree, ausers = A1.next()
                    u = tt(dve, s1, bc(s_lo[:, g:g + G], 2, 128), bc(iota_p[:, :], 1, G), ALU.is_equal, cur, sfree, t_iota)
                    v = tt(dve, a1[:, :, 0, :], bc(s_hi[:, g:g + G], 2, NS), bc(it, 1, G), ALU.is_equal, cur, afree)
                    w = dve(lambda e, a1=a1: e.tensor_scalar(a1[:, :, 1, :], a1[:, :, 0, :], pcol[:, 0:1], None, ALU.mult), v)
                    v = tt(dve, a1[:, :, 0, :], a1[:, :, 0, :], bc(tile_no[:, c, g:g + G], 2, NS), ALU.mult, w)
                    for n in range(G):
                        m = mm(mp, s1[:, n, :], a1[:, n, :, :], c == 0 and g == 0 and n == 0, c == CH - 1 and g == NT - G and n == G - 1,
                               u, v, everything, mark=(n == G - 1))
                    susers.append(m)
                    ausers.append(m)
                    cur = v
            rf, pad = area(NS), area(NS)
            slot_no = area(NS)
            t_sn = iota(slot_no, [[128, NS]], CH * NT * 128, 1, ready)
            r_i = area(NS).bitcast(i32)
            cur = dve(lambda e: e.tensor_scalar(pad, mp[:, 0, :], 1.0, None, ALU.is_lt), m)
            cur = dve(lambda e: e.tensor_scalar(rf, mp[:, 0, :], 128.0, -128.0, ALU.mult, ALU.add), cur)
            cur = tt(dve, rf, rf, mp[:, 1, :], ALU.add, cur)
            cur = copy(dve, r_i, rf, cur)
            t_gi = dve(lambda e: e.tensor_scalar(gi, r_i, T - 1, None, ALU.bitwise_and), cur)
            cur = tt(dve, slot_no, slot_no, rf, ALU.subtract, cur, t_sn)
            cur = tt(dve, slot_no, slot_no, pad, ALU.mult, cur)
            cur = tt(dve, rf, rf, slot_no, ALU.add, cur)
            t_yi = copy(dve, yi, rf, cur)

            area = Area(base)
            HIN = area.ring(3, 2 * D, dt=f16)
            HTT = area.ring(2, 4, 128, dt=f16)
            UP = area.ring(2, 1024)
            UPT = area.pairs(1 if l else 2, 8, 128)
            YO = area.ring(2, D)
            if l == 0:
                st_, hv_ = area.ring(2, 1024), area.pairs(2, 1024)
            everything = now()
            for q in (act, dve, pe, pool, sp):
                q.wait(everything, t_hb)
            wide = Ring([ps[0], ps[1], ps[2], ps[3]])
            trb = Ring([ps[6], ps[7]])
            yb = Ring([ps[4], ps[5]])
            l_hi = [sem(f"l_hi{l}_{i}") for i in range(3)]
            l_yo = [sem(f"l_yo{l}_{i}") for i in range(2)]
            regs = {}

            def reg(j):
                def f(e):
                    regs.pop(j - 3, None)
                    regs[j] = e.value_load(ei[0:1, j:j + 1], min_val=0, max_val=(E - 1) * span)
                pe.wait(t_ei, t_w)
                pe.items.append(f)

            def mm_w(out, lhs, j, at, n, start, stop, *after, mark=False):
                for p, (m, w) in enumerate(((0, 0), (0, 1), (1, 0))):
                    r = pe(lambda e, m=m, w=w, p=p: e.matmul(
                        out, lhs[m], BIG16[:, bass.ds(regs[j] + (w * nslab * 2048 + at), n)],
                        start=start and p == 0, stop=stop and p == 2, skip_group_check=True),
                        *after, mark=mark and p == 2)
                return r

            def fetch(j):
                h, hfree, husers = HIN.next()
                return h, pool.gather(l_hi[j % 3], h, HB, gi[:, j:j + 1], t_gi, t_hb, hfree), husers

            def turn(j, h, a, husers):
                b16, m, busers = rows_T2(h, a)
                husers.append(m)
                ht, tfree, tusers = HTT.next()
                a = copy(act, ht, b16, m, tfree)
                busers.append(a)
                return ht, a, tusers

            def rows_T2(src, *after):
                bk, bfree, busers = trb.next()
                b16 = shaped(bk[:, 0:256].bitcast(f16), (4, 128))
                for k in range(4):
                    m = tp16(b16[:, k, :], src[:, k * 128:(k + 1) * 128], *after, bfree, mark=(k == 3))
                return b16, m, busers

            def up(j, hf, ht, a, u, ufree):
                bks = []
                for w in range(2 if gated else 1):
                    bk, bfree, busers = wide.next()
                    for k in range(2):
                        m = mm_w(bk[:, :], (ht[:, k, :], ht[:, 2 + k, :]), j, 2048 * w + 1024 * k + 512 * hf, 512,
                                 k == 0, k == 1, a, bfree, mark=(k == 1))
                    bks.append((bk, m, busers))
                us = u[:, hf * 512:hf * 512 + 512]
                bk, m, busers = bks[0]
                s_ = act(lambda e: e.activation(us, bk[:, :], ACT.Silu if gated else ACT.Gelu), m, ufree)
                busers.append(s_)
                if gated:
                    bk2, m2, busers2 = bks[1]
                    s_ = tt(dve, us, us, bk2[:, :], ALU.mult, s_, m2)
                    busers2.append(s_)
                return s_, bks[-1][1]

            def u_T(u, parts, uusers):
                ut, tfree, tusers = UPT.next()
                cp = []
                for q in range(2):
                    bk, bfree, busers = trb.next()
                    for n in range(4):
                        m = tp(bk[:, n * 128:(n + 1) * 128], u[:, (4 * q + n) * 128:(4 * q + n + 1) * 128],
                               parts[q], bfree, mark=(n == 3))
                    uusers.append(m)
                    s_ = split([h[:, 4 * q:4 * q + 4, :] for h in ut], bk[:, :].rearrange("p (j n) -> p j n", j=4),
                               dve, m, tfree)
                    busers.extend(s_)
                    cp.append(s_)
                return ut, cp, tusers

            def down(j, ut, cp, tusers):
                bk, bfree, busers = yb.next()
                for n in range(8):
                    m = mm_w(bk[:, 0:256], [h[:, n, :] for h in ut], j, (nslab - 1) * 2048 + 256 * n, 256, n == 0, n == 7,
                             cp[n // 4], bfree, mark=(n == 7))
                tusers.append(m)
                y, yfree, yusers = YO.next()
                a = copy(act, y, bk[:, 0:256], m, yfree)
                busers.append(a)
                yusers.append(pool.scatter(l_yo[j % 2], YT, yi[:, j:j + 1], y, a, t_yi))

            fetched = [fetch(0), fetch(1)]
            turned = turn(0, *fetched[0])
            reg(0)
            late = None
            n_conv = len(slab_list(1))
            for j in range(NS):
                ht, t_ht, tusers = turned
                if j + 1 < NS:
                    reg(j + 1)
                u, ufree, uusers = UP.next()
                p0, _ = up(j, 0, ht, t_ht, u, ufree)
                if late:
                    got = u_T(*late)
                p1, m = up(j, 1, ht, t_ht, u, ufree)
                tusers.append(m)
                if j + 2 < NS:
                    fetched.append(fetch(j + 2))
                if j + 1 < NS:
                    turned = turn(j + 1, *fetched[j + 1])
                if late:
                    down(j - 1, *got)
                late = (u, (p0, p1), uusers)
                if l == 0 and j % 4 == 0 and j // 4 < n_conv:
                    convert(1, j // 4, st_, hv_, pool)
            got = u_T(*late)
            down(NS - 1, *got)
            t_ys = [(s_, s_.n) for s_ in l_yo]
            area = Area(base)
            YI = area.ring(3, CH, 4, D)
            l_yi = [sem(f"l_yi{l}_{i}") for i in range(3)]
            gb = Ring([ps[0], ps[1]])
            everything = now()
            outs = []
            YTv = YT[0:CH * T, :].rearrange("(c t p) d -> p c t d", c=CH, p=128)
            for g in range(0, NT, 4):
                gk, gfree, gusers = gb.next()
                t_g = gates(l, 1, gk, g // 4, gfree, everything)
                y4, yfree, yusers = YI.next()
                n = g // 4 % 3
                for c in range(CH):
                    t_y4 = sp.dma(l_yi[n], y4[:, c], YTv[:, c, g:g + 4, :], t_ys, yfree, everything)
                for i in range(g, g + 4):
                    y = y4[:, 0, i - g, :]
                    a = dve(lambda e, y=y, i=i: e.tensor_scalar(y, y, GV[0][:, i:i + 1], None, ALU.mult), t_y4)
                    if CH == 2:
                        y2 = y4[:, 1, i - g, :]
                        a = dve(lambda e, y=y, y2=y2, i=i: e.scalar_tensor_tensor(
                            out=y, in0=y2, scalar=GV[1][:, i:i + 1], in1=y, op0=ALU.mult, op1=ALU.add), a)
                    a = tt(dve, y, y, gk[:, 0:256], ALU.mult, a, t_g)
                    a = tt(dve, X[:, i, :], X[:, i, :], y, ALU.add, a)
                    outs.append(a)
                gusers.append(a)
                yusers.append(a)
            return outs

        if phases >= 2:
            before = now()
            phase_sems(1)
            t_x = moe(0, 4, 2, rw_in, rb_in, True, before, t_x, t_conv)
            t_conv = [[(s_, s_.n) for s_ in sv_sem]]

        if phases >= 3:
            before = now()
            phase_sems(2)
            area = Area(0)
            HFh, HFl = area.pair(2, 2048)
            QK = area.ring(2, 16, 256)
            PB = area.ring(3, 2, 16, 64)
            PV = area.ring(2, 2, 1024)
            ET = area.ring(4, 2, 16, 16)
            SM = area.ring(4, 2, 2, 16)
            OB = area.ring(2, 16, 64)
            Wq, Wu = area.pair(2, 1024), area.pair(2, 256)
            wst = area(2, 1024)
            wsu = area(2, 256)
            xnr, vr1 = area.ring(3, D), area.ring(2, 2, 128)
            l_w1 = sem("l_w1")
            sp.dma(l_w1, wst, qkvw_in.rearrange("(k p) n -> p k n", p=128), before)
            t_w1 = sp.dma(l_w1, wsu, wout_in.rearrange("(k p) n -> p k n", p=128), before)
            for q in (dve, act, pool, pe):
                q.wait(before)
            flat = "p a b -> p (a b)"
            t_wq = split([w.rearrange(flat) for w in Wq], wst.rearrange(flat), pool, t_w1)
            t_wq += split([w.rearrange(flat) for w in Wu], wsu.rearrange(flat), pool, t_w1)
            st4 = []
            for g4 in range(0, NT, 8):
                for i in range(g4, g4 + 8):
                    a = tile_stats(i, t_x[i])
                st4.append(rstd_of(g4, g4 + 8, a))
            OW = dram("OW", [T * 4, 64])
            tr = Ring([ps[6], ps[7]])
            qb = Ring([ps[0], ps[1]])
            sb_ = Ring([ps[2], ps[3], ps[4], ps[5]])
            l_ow = [sem(f"l_ow{i}") for i in range(2)]

            def project(bh, ci, ends):
                qk, free, qusers = QK.next()
                t_cp = []
                for h in range(16):
                    bk, bfree, busers = qb.next()
                    for k in range(2):
                        m = mm3(bk[:, 0:256], (HFh[:, k, 128 * h:128 * h + 128], HFl[:, k, 128 * h:128 * h + 128]),
                                [w[:, k, 256 * ci:256 * ci + 256] for w in Wq], k == 0, k == 1,
                                ends, bfree, t_wq, mark=(k == 1))
                    a = copy(act, qk[:, h, :], bk[:, 0:256], m, free)
                    busers.append(a)
                    t_cp.append(a)
                return qk, t_cp, qusers, m

            def scores(qk, t_cp, q2):
                pb, pfree, pusers = PB.next()
                ms = []
                for q in range(2):
                    ms.append(tt(pool, pb[:, q], bc(qk[:, 2 * q2 + q, 0:64], 1, 16), qk[:, :, 64:128], ALU.mult, t_cp, pfree))
                bk, bfree, busers = sb_.next()
                pv = pb.rearrange("p q k (f d) -> p (q k f) d", d=4)
                for d in range(4):
                    m = mm(bk[:, :], ident[:, :], pv[:, :, d], d == 0, d == 3, ms, bfree, mark=(d == 3))
                pusers.append(m)
                return bk, m, busers

            def soft(bk, m, busers):
                s4 = bk[:, :].rearrange("p (q k f) -> p q k f", q=2, k=16)
                sm, sfree, susers = SM.next()
                et, efree, eusers = ET.next()
                a = dve(lambda e: e.tensor_reduce(sm[:, 0], s4.rearrange("p q k f -> p q f k"), AX.X, ALU.max), m, sfree)
                a = tt(dve, et, s4, bc(sm[:, 0], 2, 16), ALU.subtract, a, efree)
                busers.append(a)
                a = act(lambda e: e.activation(et, et, ACT.Exp, scale=0.5), a)
                return et, eusers, sm, susers, a

            def values(qk, q2, ob, ofree, et, eusers, sm, susers, a):
                s_ = dve(lambda e: e.tensor_reduce(sm[:, 1], et.rearrange("p q k f -> p q f k"), AX.X, ALU.add), a)
                s_ = dve(lambda e: e.reciprocal(sm[:, 1], sm[:, 1]), s_)
                pv, pfree, pusers = PV.next()
                ms = []
                for q in range(2):
                    ms.append(tt(dve, pv[:, q].rearrange("p (f d k) -> p f d k", f=16, d=4),
                                 bc(et[:, q].rearrange("p k f -> p f k"), 2, 4),
                                 qk[:, :, 128:192].rearrange("p k (f d) -> p f d k", d=4), ALU.mult, a, pfree))
                eusers.append(ms[-1])
                o2 = ob[:, 2 * q2:2 * q2 + 2, :]
                r = dve(lambda e: e.tensor_reduce(o2, pv.rearrange("p q (n k) -> p (q n) k", k=16), AX.X, ALU.add), ms, ofree)
                pusers.append(r)
                r = tt(dve, o2.rearrange("p q (f d) -> p q f d", d=4), o2.rearrange("p q (f d) -> p q f d", d=4),
                       bc(sm[:, 1], 3, 4), ALU.mult, r, s_)
                susers.append(r)
                return r

            for bh in range(2):
                if bh:
                    for q in (act, pool):
                        q.wait(t_prj)

                def place(n, v):
                    def at(h_):
                        return h_.rearrange("p k (h b t) -> p k h b t", h=16, b=4)[:, :, 4 * (n % 4):4 * (n % 4) + 4, n // 4, :]
                    return at(HFh), at(HFl), v.rearrange("p k (h t) -> p k h t", h=4)
                ends = norm_T(1, place, (xnr, vr1), tr, lambda i: st4[i // 8], range(16 * bh, 16 * bh + 16))
                nxt = project(bh, 0, ends)
                for ci in range(4):
                    qk, t_cp, qusers, t_prj = nxt
                    ob, ofree, ousers = OB.next()
                    sc = [scores(qk, t_cp, 0), scores(qk, t_cp, 1)]
                    sf = [soft(*sc[0])]
                    if ci < 3:
                        nxt = project(bh, ci + 1, ends)
                    for q2 in range(8):
                        if q2 + 2 < 8:
                            sc.append(scores(qk, t_cp, q2 + 2))
                        if q2 + 1 < 8:
                            sf.append(soft(*sc[q2 + 1]))
                        a = values(qk, q2, ob, ofree, *sf[q2])
                    a = tt(dve, ob, ob, qk[:, :, 192:256], ALU.mult, a)
                    qusers.append(a)
                    for b in range(4):
                        r0 = (ci * 8 + bh * 4 + b) * 512
                        ousers.append(sp.dma(l_ow[ci % 2], OW[r0:r0 + 512, :].rearrange("(h t) f -> t h f", t=32),
                                             ob[32 * b:32 * b + 32, :, :], a))
            t_ow = [(s_, s_.n) for s_ in l_ow]
            everything = now()
            area = Area(0)
            OI, OIP, OIT, YG = area.ring(3, D), area.ring(2, 2, D, dt=f16), area.ring(2, 4, 128, dt=f16), area.ring(2, D)
            for q in (dve, act, pool, pe, sp):
                q.wait(everything)
            OWv = OW.rearrange("(t p r) f -> t p (r f)", p=128, r=4)
            l_oi = [sem(f"l_oi{i}") for i in range(3)]
            gb = Ring([ps[2], ps[3]])
            t_x2 = []
            for i in range(NT):
                if i % 4 == 0:
                    gk, gfree, gusers = gb.next()
                    t_g = gates(1, 0, gk, i // 4, gfree)
                    yg4 = []
                oi, free, users = OI.next()
                a = sp.dma(l_oi[i % 3], oi, OWv[i], t_ow, free)
                op_, pfree, pusers = OIP.next()
                s_ = split((op_[:, 0, :], op_[:, 1, :]), oi, pool, a, pfree)
                users.extend(s_)
                bk, bfree, busers = tr.next()
                b16 = shaped(bk[:, 0:256].bitcast(f16), (4, 128))
                fl = op_.rearrange("p a b -> p (a b)")
                for k in range(4):
                    m = tp16(b16[:, k, :], fl[:, k * 128:(k + 1) * 128], s_, bfree, mark=(k == 3))
                pusers.append(m)
                ot, tfree, tusers = OIT.next()
                a = copy(act, ot, b16, m, tfree)
                busers.append(a)
                bk, bfree, busers = qb.next()
                for k in range(2):
                    m = mm3(bk[:, 0:256], (ot[:, k, :], ot[:, 2 + k, :]), [w[:, k, :] for w in Wu], k == 0, k == 1,
                            a, bfree, mark=(k == 1))
                tusers.append(m)
                yg, yfree, yusers = YG.next()
                y0 = copy(act, yg, bk[:, 0:256], m, yfree)
                busers.append(y0)
                y = tt(dve, yg, yg, gk[:, 0:256], ALU.mult, y0, t_g)
                if i % 4 == 3:
                    gusers.append(y)
                y = tt(dve, X[:, i, :], X[:, i, :], yg, ALU.add, y)
                yusers.append(y)
                t_x2.append(y)
            t_x = t_x2

        if phases >= 4:
            before = now()
            phase_sems(3)
            t_x = moe(1, 8, 1, wr_in, br_in, False, before, t_x, t_conv)

        l_o = sem("l_o")
        ov = out.rearrange("(t p) d -> p t d", p=128)
        for i in range(0, NT, 4):
            t_o = sp.dma(l_o, ov[:, i:i + 4, :], X[:, i:i + 4, :], [t_x[j] for j in range(i, i + 4)])
        sp.wait(t_o)

        block = ctx.enter_context(nc.Block())
        block.sync(sp.play)
        block.gpsimd(pool.play)
        block.scalar(act.play)
        block.vector(dve.play)
        block.tensor(pe.play)


def lay_out(i, np):
    a = {k: np.ascontiguousarray(v) for k, v in i.items()}
    return {
        "x": a["L0_attn_query"].reshape(T, D),
        "wqk": np.ascontiguousarray(np.concatenate([a["L0_attn_W_Q"][:, :, 0], a["L0_attn_W_K"][:, :, 0]]).T),
        "wv": np.ascontiguousarray(a["L0_attn_W_V"].transpose(1, 0, 2).reshape(D, 1024)),
        "wo": np.ascontiguousarray(a["L0_attn_W_O"].transpose(2, 1, 0).reshape(1024, D)),
        "rw": a["L0_ffn_router_w"], "rb": a["L0_ffn_router_b"],
        "w1": a["L0_ffn_w1"], "w3": a["L0_ffn_w3"], "w2": a["L0_ffn_w2"],
        "c0": a["L0_c"], "m0": a["L0_wmod"],
        "qkvw": a["L1_attn_w_qkvw"], "wout": a["L1_attn_w_out"],
        "wr": a["L1_ffn_Wr"], "br": a["L1_ffn_br"], "v1": a["L1_ffn_W1"], "v2": a["L1_ffn_W2"],
        "c1": a["L1_c"], "m1": a["L1_wmod"],
    }


def kernel(**inputs):
    import numpy as np
    import concourse.bacc as bacc
    from concourse.bass_utils import run_bass_kernel_spmd

    nc = bacc.Bacc("TRN2", target_bir_lowering=False, num_devices=1)
    arrays = {f"in_{k}": v for k, v in lay_out(inputs, np).items()}
    args = [nc.dram_tensor(k, v.shape, mybir.dt.from_np(v.dtype), kind="ExternalInput").ap() for k, v in arrays.items()]
    out = nc.dram_tensor("out_0", (T, D), fp32, kind="ExternalOutput").ap()
    program(nc, *args, out)
    r = run_bass_kernel_spmd(nc, [arrays], core_ids=[0])
    return r.results[0]["out_0"].reshape(B, S, D)
```

```python
import math

import concourse.bass as bass
from concourse import mybir

fp32 = mybir.dt.float32
i32 = mybir.dt.int32
f16 = mybir.dt.float16
ALU = mybir.AluOpType
ACT = mybir.ActivationFunctionType
AX = mybir.AxisListType

B, S, D = 8, 512, 256
T = B * S
NT = T // 128
PI = math.pi
BIGW = 39680


class Sem:

    def __init__(self, sem):
        self.sem, self.n = sem, 0

    def up(self, by):
        self.n += by
        return (self, self.n)


class Queue:

    def __init__(self, name):
        self.name, self.items, self.done, self.seen = name, [], None, {}

    def wait(self, *tokens):
        most = {}

        def collect(ts):
            for t in ts:
                if isinstance(t, list):
                    collect(t)
                elif t is not None:
                    most[t[0]] = max(most.get(t[0], 0), t[1])
        collect(tokens)
        for sem, n in most.items():
            if self.seen.get(sem, 0) < n:
                self.seen[sem] = n
                self.items.append(lambda e, s=sem.sem, n=n: e.wait_ge(s, n))

    def __call__(self, f, *after, mark=True):
        self.wait(*after)
        if not mark:
            self.items.append(f)
            return None
        t = self.done.up(1)
        self.items.append(lambda e, f=f, s=t[0].sem: f(e).then_inc(s, 1))
        return t

    def dma(self, sem, out, in_, *after):
        self.wait(*after)
        t = sem.up(16)
        self.items.append(lambda e: e.dma_start(out, in_).then_inc(sem.sem, 16))
        return t

    def scatter(self, sem, out, idx, in_, *after):
        self.wait(*after)
        t = sem.up(16)
        self.items.append(lambda e: e.indirect_dma_start(
            out, bass.IndirectOffsetOnAxis(idx, 0), in_, None).then_inc(sem.sem, 16))
        return t

    def gather(self, sem, out, in_, idx, *after):
        self.wait(*after)
        t = sem.up(16)
        self.items.append(lambda e: e.indirect_dma_start(
            out, None, in_, bass.IndirectOffsetOnAxis(idx, 0)).then_inc(sem.sem, 16))
        return t

    def play(self, e):
        for f in self.items:
            f(e)


class Ring:

    def __init__(self, bufs):
        self.bufs, self.free, self.i = bufs, [[] for _ in bufs], -1

    def next(self):
        self.i = (self.i + 1) % len(self.bufs)
        free, self.free[self.i] = self.free[self.i], []
        return self.bufs[self.i], free, self.free[self.i]


def program(nc, x_in, wqk_in, wv_in, wo_in, rw_in, rb_in, w1_in, w3_in, w2_in, c0_in, m0_in,
            qkvw_in, wout_in, wr_in, br_in, v1_in, v2_in, c1_in, m1_in, out, phases=4):
    from contextlib import ExitStack
    ctx = ExitStack()
    with ctx:
        def sb(name, shape, dt=fp32):
            return ctx.enter_context(nc.sbuf_tensor(name, shape, dt))

        def sem(name):
            return Sem(ctx.enter_context(nc.semaphore(name)))

        X = sb("X", [128, NT, D])
        BIG = sb("BIG", [128, BIGW])
        BIG16 = BIG[:, :].bitcast(f16)
        ident = sb("ident", [128, 128])
        ident16 = sb("ident16", [128, 128], f16)
        tri = sb("tri", [128, 128], f16)
        atri = sb("atri", [128, 128], f16)
        stri = sb("stri", [128, 128], f16)
        ones = sb("ones", [128, 128], f16)
        sel = sb("sel", [8, 8, 128])
        MOD = sb("MOD", [8, 2, 6 * D])
        modT = sb("modT", [128, 2, 4, 8])
        stat = sb("stat", [128, NT, 2])
        rstd = sb("rstd", [128, NT])
        half_pi = sb("half_pi", [128, 1])
        bnst = sb("bnst", [128, 4, 6])
        pcol = sb("pcol", [128, 1])
        iota_p = sb("iota_p", [128, 128])
        tile_no = sb("tile_no", [128, 2, NT])

        ps = [ctx.enter_context(nc.psum_tensor(f"ps{i}", [128, 512], fp32)) for i in range(8)]

        def dram(name, shape, dt=fp32):
            return nc.dram_tensor(name, shape, dt, kind="Internal").ap()

        def shaped(v, shape):
            if len(shape) == 1:
                return v
            names = "abcdef"[:len(shape)]
            return v.rearrange(f"p ({' '.join(names)}) -> p {' '.join(names)}",
                               **{k: s for k, s in zip(names[1:], shape[1:])})

        def view(off, *shape, dt=None, parts=128):
            n = math.prod(shape)
            words = n // 2 if dt == f16 else n
            assert off + words <= BIGW, (off, shape)
            v = BIG[0:parts, off:off + words]
            return shaped(v.bitcast(dt) if dt is not None else v, shape)

        class Area:

            def __init__(self, start):
                self.at = start

            def __call__(self, *shape, dt=None, parts=128):
                v = view(self.at, *shape, dt=dt, parts=parts)
                n = math.prod(shape)
                self.at += (n + 1) // 2 if dt == f16 else n
                return v

            def ring(self, n, *shape, dt=None):
                return Ring([self(*shape, dt=dt) for _ in range(n)])

            def pair(self, *shape):
                return self(*shape, dt=f16), self(*shape, dt=f16)

            def pairs(self, n, *shape):
                return Ring([self.pair(*shape) for _ in range(n)])

        pe, dve, act, pool, sp = (Queue(n) for n in ("pe", "dve", "act", "pool", "sp"))

        def phase_sems(n):
            for q in (pe, dve, act, pool):
                q.done = sem(f"{q.name}_{n}")

        def now(*queues):
            return [(q.done, q.done.n) for q in (queues or (pe, dve, act, pool)) if q.done.n]

        def mm(out, lhsT, rhs, start, stop, *after, mark=False):
            return pe(lambda e: e.matmul(out, lhsT, rhs, start=start, stop=stop, skip_group_check=True),
                      *after, mark=mark)

        def mm3(out, lhs, rhs, start, stop, *after, mark=False):
            mm(out, lhs[0], rhs[0], start, False, *after)
            mm(out, lhs[0], rhs[1], False, False)
            return mm(out, lhs[1], rhs[0], False, stop, mark=mark)

        def tp(out, in_, *after, mark=False, n=128):
            return pe(lambda e: e.transpose(out, in_, ident[0:n, 0:n]), *after, mark=mark)

        def tp16(out, in_, *after, mark=False):
            return pe(lambda e: e.transpose(out, in_, ident16[:, :]), *after, mark=mark)

        def copy(q, out, in_, *after):
            if q is act:
                return act(lambda e: e.activation(out, in_, ACT.Copy), *after)
            return q(lambda e: e.tensor_copy(out, in_), *after)

        def tt(q, out, a, b, op, *after):
            return q(lambda e: e.tensor_tensor(out, a, b, op), *after)

        def split(pair, src, q_lo, *after):
            h = copy(act, pair[0], src, *after)
            return [h, tt(q_lo, pair[1], src, pair[0], ALU.subtract, h)]

        def bank(i, *shape, dt=None):
            n = math.prod(shape)
            if dt == f16:
                return shaped(ps[i][:, 0:n // 2].bitcast(f16), shape)
            return shaped(ps[i][:, 0:n], shape)

        def bc(ap, axis, n):
            a = ap.unsqueeze(axis)
            shape = list(a.shape)
            shape[axis] = n
            return a.broadcast_to(shape)

        def pipeline(n, stages, begin=0, end=None):
            steps = n + len(stages) - 1
            for t in range(begin, steps if end is None else min(end, steps)):
                for s in reversed(range(len(stages))):
                    if 0 <= t - s < n:
                        stages[s](t - s)

        phase_sems(0)

        l_x = [sem(f"l_x{i}") for i in range(4)]
        xt = []
        xv = x_in.rearrange("(t p) d -> p t d", p=128)
        l_c = sem("l_c")
        area = Area(22912)
        WM = area(2, 2, 6 * D)
        CS = area(2, D, parts=8)
        cT = area(2, 2, 8)
        GT = area(2, 2, D, parts=8)
        mod_end = area.at
        sp.dma(l_c, CS[:, 0, :], c0_in)
        sp.dma(l_c, CS[:, 1, :], c1_in)
        for i in range(4):
            xt.append(sp.dma(l_x[i], X[:, 8 * i:8 * i + 8, :], xv[:, 8 * i:8 * i + 8, :]))
            if i == 0:
                sp.dma(l_c, WM[:, 0], m0_in.rearrange("(k p) n -> p k n", p=128))
                t_c = sp.dma(l_c, WM[:, 1], m1_in.rearrange("(k p) n -> p k n", p=128))

        t = [pool(lambda e, a=a, v=v: e.memset(a, v)) for a, v in
             ((ident[:, :], 0.0), (tri[:, :], 1.0), (stri[:, :], 1.0), (atri[:, :], 1.0),
              (ones[:, :], 1.0), (sel[:, :, :], 0.0), (half_pi[:, :], PI / 2))]

        def affine(ap, cmp, fill, base, pattern, cm, *after):
            return pool(lambda e: e.affine_select(out=ap, in_=ap, compare_op=cmp, fill=fill, base=base,
                                                  pattern=pattern, channel_multiplier=cm), *after)

        def iota(ap, pattern, base=0, cm=0, *after):
            return pool(lambda e: e.iota(ap, pattern, base=base, channel_multiplier=cm,
                                         allow_small_or_imprecise_dtypes=True), *after)
        t_id = affine(ident[:, :], ALU.not_equal, 1.0, 0, [[-1, 128]], 1, t[0])
        t_tri = affine(tri[:, :], ALU.is_ge, 0.0, 0, [[1, 128]], -1, t[1])
        t_stri = affine(stri[:, :], ALU.is_ge, 0.0, -1, [[1, 128]], -1, t[2])
        t_atri = affine(atri[:, :], ALU.is_ge, 0.0, -1, [[-1, 128]], 1, t[3])
        t_sel = affine(sel[:, :, :], ALU.not_equal, 1.0, 0, [[-1, 8], [0, 128]], 1, t[5])
        t_id16 = copy(pool, ident16[:, :], ident[:, :], t_id)
        iota(pcol[:, :], [[0, 1]], 0, 1)
        iota(iota_p[:, :], [[1, 128]])
        t_iota = iota(tile_no[:, :, :], [[NT, 2], [1, NT]], 1)
        t_ones, t_hp = t[4], t[6]

        t_silu = act(lambda e: e.activation(CS, CS, ACT.Silu), t_c)
        pT = bank(0, 2, 2, 8)
        for l in range(2):
            for k in range(2):
                t_tp = tp(pT[:, l, k, :], CS[:, l, k * 128:(k + 1) * 128], t_silu, t_id, mark=True, n=8)
        t_cT = copy(dve, cT, pT, t_tp)
        t_prev = None
        modt = []
        for l in range(2):
            for j in range(3):
                for k in range(2):
                    t_m = mm(ps[1 + j][0:8, :], cT[:, l, k, :], WM[:, l, k, 512 * j:512 * j + 512],
                             k == 0, k == 1, t_cT, t_prev, mark=(k == 1))
            for j in range(3):
                t_prev = copy(dve, MOD[:, l, 512 * j:512 * j + 512], ps[1 + j][0:8, :], t_m)
            pc = bank(4 + l, 4, 8)
            for blk in range(4):
                for k in range(2):
                    t_m = mm(pc[:, blk, :], WM[:, l, k, 128 * blk:128 * blk + 128], cT[:, l, k, :],
                             k == 0, k == 1, mark=(k == 1))
            t_mt = copy(dve, modT[:, l, :, :], pc, t_m)
            t_mt = dve(lambda e, l=l: e.tensor_scalar(modT[:, l, 2:4, :], modT[:, l, 2:4, :], 1.0, None, ALU.add), t_mt)
            modt.append(t_mt)
        gview = MOD.rearrange("b l (u v d) -> b l u v d", u=2, v=3)[:, :, :, 2, :]
        cview = MOD.rearrange("b l (u v d) -> b l u v d", u=2, v=3)[:, :, :, 1, :]
        for l in range(2):
            g = gview[:, l]
            t1 = dve(lambda e, g=g, l=l: e.tensor_scalar(GT[:, l], g, -1.0, None, ALU.mult), t_prev)
            t1 = tt(dve, GT[:, l], GT[:, l], g, ALU.max, t1)
            t1 = dve(lambda e, g=g, l=l: e.tensor_scalar(GT[:, l], GT[:, l], 0.25, None, ALU.max), t1)
            t2 = dve(lambda e, g=g: e.tensor_scalar(g, g, 0.0, 2.0, ALU.is_ge, ALU.mult), t1)
            t2 = dve(lambda e, g=g, l=l: e.scalar_tensor_tensor(out=g, in0=g, scalar=-1.0, in1=GT[:, l],
                                                                op0=ALU.add, op1=ALU.mult), t2)
            t_mod = dve(lambda e, l=l: e.tensor_scalar(cview[:, l], cview[:, l], 1.0, None, ALU.add), t2)
        t_mod_done = now(pe, dve, act)

        bn_last = [None] * 4

        def tile_stats(i, *ready):
            r = i % 4
            a = dve(lambda e: e.bn_stats(bnst[:, r, :], X[:, i, :]), bn_last[r], *ready)
            bn_last[r] = dve(lambda e: e.bn_aggr(stat[:, i, :], bnst[:, r, :]), a)
            return bn_last[r]

        def rstd_of(i, j, *ready):
            a = dve(lambda e: e.tensor_scalar(rstd[:, i:j], stat[:, i:j, 1], 1e-5, None, ALU.add), *ready)
            a = act(lambda e: e.activation(rstd[:, i:j], rstd[:, i:j], ACT.Sqrt), a)
            return dve(lambda e: e.reciprocal(rstd[:, i:j], rstd[:, i:j]), a)

        def xnorm(dst, i, *after):
            return dve(lambda e: e.tensor_scalar(dst, X[:, i, :], stat[:, i, 0:1], rstd[:, i:i + 1],
                                                 ALU.subtract, ALU.mult), *after)

        def settled(i, y, t_rstd):
            a = tile_stats(i, y)
            if i % 8 == 7:
                t_rstd.append(rstd_of(i - 7, i + 1, a))

        def norm_T(l, place, rings, banks, t_stats, tiles, ends):
            xn_ring, v_ring = rings
            got = {}

            def first(n):
                xn, free, users = xn_ring.next()
                got[n] = xn, xnorm(xn, tiles[n], t_stats(tiles[n]), free), users

            def second(n):
                xn, a, users = got[n]
                bk, bfree, busers = banks.next()
                for k in range(2):
                    m = tp(bk[:, k * 128:(k + 1) * 128], xn[:, k * 128:(k + 1) * 128], a, bfree, mark=(k == 1))
                users.append(m)
                got[n] = bk, m, busers

            def third(n):
                bk, m, busers = got[n]
                b = tiles[n] // 4
                v, vfree, vusers = v_ring.next()
                for k in range(2):
                    a = act(lambda e, k=k: e.activation(
                        v[:, k, :], bk[:, k * 128:(k + 1) * 128], ACT.Identity,
                        bias=modT[:, l, k, b:b + 1], scale=modT[:, l, 2 + k, b:b + 1]), m, modt[l], vfree)
                busers.append(a)
                got[n] = v, a, vusers

            def fourth(n):
                v, a, vusers = got.pop(n)
                hi, lo, src = place(n, v)
                a = copy(act, hi, src, a)
                a = tt(pool, lo, src, hi, ALU.subtract, a)
                vusers.append(a)
                ends.append(a)

            return [first, second, third, fourth]

        def gates(l, which, bk, b, *after):
            return mm(bk[:, 0:256], sel[0:8, b, :], MOD[0:8, l, (2 + 3 * which) * D:(3 + 3 * which) * D],
                      True, True, t_mod, t_sel, *after, mark=True)

        def slab_list(l):
            E, ins = ((4, ((w1_in, 2), (w3_in, 2), (w2_in, 8))), (8, ((v1_in, 2), (v2_in, 8))))[l]
            return [(x, n, w[x].rearrange("(k p) n -> p k n", p=128), k) for x in range(E) for n, (w, k) in enumerate(ins)]

        WD = [dram("WD0", [128, 4 * 3 * 4096], f16), dram("WD1", [128, 8 * 2 * 4096], f16)]
        st_sem = [sem(f"l_st{i}") for i in range(2)]
        sv_sem = [sem(f"l_sv{i}") for i in range(2)]
        conv_n = [0]

        def converter(l, stage, halves, q_lo):
            nslab = (3, 2)[l]
            todo = [(*slab, hf) for slab in slab_list(l) for hf in range(2)]
            got = {}

            def load(c):
                x, n, src, k, hf = todo[c]
                st, free, users = stage.next()
                got[c] = st, sp.dma(st_sem[c % 2], shaped(st, (k // 2, 2048 // k)),
                                    src[:, hf * k // 2:(hf + 1) * k // 2, :], free), users

            def step(c):
                if c == 0:
                    load(0)
                if c + 1 < len(todo):
                    load(c + 1)
                x, n, src, k, hf = todo[c]
                st, a, users = got.pop(c)
                pr, pfree, pusers = halves.next()
                s_ = split(pr, st, q_lo, a, pfree)
                users.extend(s_)
                for m in range(2):
                    at = (x * 2 * nslab + m * nslab + n) * 2048 + hf * 1024
                    pusers.append(sp.dma(sv_sem[c % 2], WD[l][:, at:at + 1024], pr[m], s_))

            return [lambda c=c: step(c) for c in range(len(todo))]

        area = Area(0)
        hTh, hTl = area.pair(2, T)
        QC = area(NT, 32)
        QS = area(NT, 32)
        TH = area(NT, 32)
        DN = TH[:, 0:16, :].rearrange("p a b -> p (a b)").rearrange("p (t n) -> p t n", n=16)
        D2 = TH[:, 16:32, :].rearrange("p a b -> p (a b)").rearrange("p (t n) -> p t n", n=16)
        Wqk, Wv, Wo = area.pair(2, 32), area.pair(2, 1024), area.pair(8, D)
        stage = area.ring(2, 1024)
        halves = area.pairs(2, 1024)
        xnr, vr0 = area.ring(3, D), area.ring(2, 2, 128)
        GB = area(8, D)
        lap = area.at
        assert lap <= 22912, lap
        wst = view(mod_end, 4160)
        l_w = sem("l_w")
        t_lw = sp.dma(l_w, shaped(wst[:, 0:64], (2, 32)), wqk_in.rearrange("(k p) n -> p k n", p=128))
        t_lw = sp.dma(l_w, shaped(wst[:, 64:2112], (2, 1024)), wv_in.rearrange("(k p) n -> p k n", p=128))
        t_lw = sp.dma(l_w, shaped(wst[:, 2112:4160], (8, 256)), wo_in.rearrange("(k p) n -> p k n", p=128))
        ts = []
        for q4 in range(4):
            for i in range(8 * q4, 8 * q4 + 8):
                a = tile_stats(i, xt[i // 8])
            ts.append(rstd_of(8 * q4, 8 * q4 + 8, a))
        t_w = split([w.rearrange("p a b -> p (a b)") for w in Wqk], wst[:, 0:64], dve, t_lw)
        t_w += split([w.rearrange("p a b -> p (a b)") for w in Wv], wst[:, 64:2112], dve, t_lw)
        t_w += split([w.rearrange("p a b -> p (a b)") for w in Wo], wst[:, 2112:4160], dve, t_lw)
        tr = Ring([ps[6], ps[7]])
        t_hT = []
        stages = norm_T(0, lambda n, v: (hTh[:, :, n * 128:(n + 1) * 128], hTl[:, :, n * 128:(n + 1) * 128], v),
                        (xnr, vr0), tr, lambda i: ts[i // 8], range(NT), t_hT)
        qkp = [bank(i, 16, 32) for i in range(2)]
        t_qks = []

        def hT_of(i, k):
            return hTh[:, k, i * 128:(i + 1) * 128], hTl[:, k, i * 128:(i + 1) * 128]

        def qk_of(i):
            for k in range(2):
                m = mm3(qkp[i // 16][:, i % 16, :], hT_of(i, k), (Wqk[0][:, k, :], Wqk[1][:, k, :]),
                        k == 0, k == 1, t_hT[i], t_w, t_cT, mark=(k == 1))
            t_qks.append(m)

        pipeline(NT, stages + [lambda i: None, qk_of])
        t_qk = t_qks[-1]
        t_th = [act(lambda e, j=j: e.activation(TH[:, 16 * j:16 * j + 16, :], qkp[j], ACT.Tanh), t_qk) for j in range(2)]
        t_qc = act(lambda e: e.activation(QC, TH, ACT.Sin, bias=half_pi[:, 0:1], scale=PI / 4), t_th, t_hp)
        t_qs = act(lambda e: e.activation(QS, TH, ACT.Sin, scale=PI / 4), t_th)
        area = Area(lap)
        KVF = area.ring(2, 2, 1024)
        KVP = area.pairs(3, 2, 1024)
        cks = view(area.at, 2, 2, NT, 16, dt=f16)
        TM = area.ring(2, 2, 1024)
        HT = area.pairs(2, 8, 128)
        YG = Ring(xnr.bufs[0:2])
        area_b = area.at
        for j, src, tq in ((0, QC, t_qc), (1, QS, t_qs)):
            tk = split((cks[:, 0, j], cks[:, 1, j]), src[:, :, 16:32], dve, tq, t_mod_done, t_w)
            o = bank(2 + j, 8, 4, 16)
            for m in range(2):
                s4 = cks[:, m, j].rearrange("p (b c) n -> p b c n", c=4)
                mm(o, tri[:, :], s4, m == 0, False, tk, t_tri, t_ones)
                for back in range(1, 4):
                    for b in range(8):
                        end = m == 1 and back == 3 and b == 7
                        t_cum = mm(o[:, b, back:4, :], ones[:, :], s4[:, b, 0:4 - back, :], False, end, mark=end)
        cumc = bank(2, NT, 16)
        cums = bank(3, NT, 16)
        a = tt(dve, DN, QC[:, :, 0:16], cumc, ALU.mult, t_cum)
        b_ = tt(dve, D2, QS[:, :, 0:16], cums, ALU.mult, t_cum)
        a = dve(lambda e: e.scalar_tensor_tensor(out=DN, in0=DN, scalar=1e-6, in1=D2, op0=ALU.add, op1=ALU.add), a, b_)
        a = dve(lambda e: e.reciprocal(DN, DN), a)
        b_ = tt(dve, QC[:, :, 0:16], QC[:, :, 0:16], DN, ALU.mult, a)
        t_q = tt(dve, QS[:, :, 0:16], QS[:, :, 0:16], DN, ALU.mult, a)

        t_gb = None
        for b in range(8):
            g = gates(0, 0, ps[4], b, t_mod_done, t_gb)
            t_gb = copy(dve, GB[:, b, :], ps[4][:, 0:256], g)
        vr = Ring([ps[4], ps[5]])
        vr.free = [[t_gb], []]
        tr2 = tr
        acc_free = [t_q, b_]
        t_kv0 = now(pe, dve, act)

        def heads_of(ap, n=8):
            return ap.rearrange("p (h e) -> p h e", e=64)

        def l0_values(i):
            kvf, free, users = KVF.next()
            kvp, pfree, pusers = KVP.next()
            ends = []
            for hf in range(2):
                bk, bfree, busers = vr.next()
                for k in range(2):
                    a = mm3(bk[:, :], hT_of(i, k), [w[:, k, hf * 512:hf * 512 + 512] for w in Wv],
                            k == 0, k == 1, bfree, mark=(k == 1))
                for j, q in ((0, QC), (1, QS)):
                    cut = slice(hf * 512, hf * 512 + 512)
                    f = tt(dve, heads_of(kvf[:, j, cut]), heads_of(bk[:, :]),
                           bc(q[:, i, 16 + 8 * hf:24 + 8 * hf], 2, 64), ALU.mult, a, free, t_kv0)
                    busers.append(f)
                    s_ = split((kvp[0][:, j, cut], kvp[1][:, j, cut]), kvf[:, j, cut], pool, f, pfree)
                    users.extend(s_)
                    ends.extend(s_)
            return kvp, ends, pusers

        def l0_out(i, hd, t_hd, hd_users):
            ht, hfree, husers = HT.next()
            cp = []
            for q in range(2):
                bk, bfree, busers = tr2.next()
                for j in range(4):
                    a = tp(bk[:, j * 128:(j + 1) * 128], hd[:, (4 * q + j) * 128:(4 * q + j + 1) * 128], t_hd, bfree,
                           mark=(j == 3))
                hd_users.append(a)
                s_ = split([h[:, 4 * q:4 * q + 4, :] for h in ht], bk[:, :].rearrange("p (j n) -> p j n", j=4), dve, a, hfree)
                busers.extend(s_)
                cp.append(s_)
            return ht, cp, husers

        def l0_proj(i, ht, cp, husers):
            bk, bfree, busers = vr.next()
            for j in range(8):
                m = mm3(bk[:, 0:256], [h[:, j, :] for h in ht], [w[:, j, :] for w in Wo],
                        j == 0, j == 7, cp[j // 4], bfree, mark=(j == 7))
            husers.append(m)
            yg, yfree, yusers = YG.next()
            y = tt(dve, yg, bk[:, 0:256], GB[:, i // 4, :], ALU.mult, m, yfree)
            busers.append(y)
            y = tt(dve, X[:, i, :], X[:, i, :], yg, ALU.add, y)
            yusers.append(y)
            return y

        t_x = []
        late = None
        steps = converter(0, stage, halves, pool)
        vals = [l0_values(0), l0_values(1)]
        for i in range(NT):
            kv, ends, kusers = vals[i]
            first = i % 4 == 0
            for j in range(2):
                for hf in range(2):
                    for m2 in range(2):
                        end = j == 1 and hf == 1 and m2 == 1
                        m = mm(ps[2 * j + hf][:, :], tri[:, :], kv[m2][:, j, hf * 512:hf * 512 + 512],
                               first and m2 == 0, False, ends, acc_free, mark=end)
            tm, tfree, tusers = TM.next()
            reads = []
            for j, q in ((0, QC), (1, QS)):
                for hf in range(2):
                    reads.append(tt(dve, heads_of(tm[:, j, hf * 512:hf * 512 + 512]), heads_of(ps[2 * j + hf][:, :]),
                                    bc(q[:, i, 8 * hf:8 * hf + 8], 2, 64), ALU.mult, m, tfree))
            if late is not None:
                got = l0_out(*late)
            if i + 2 < NT:
                vals.append(l0_values(i + 2))
            acc_free = reads
            if i % 4 != 3:
                for j in range(2):
                    for hf in range(2):
                        for m2 in range(2):
                            end = j == 1 and hf == 1 and m2 == 1
                            m = mm(ps[2 * j + hf][:, :], atri[:, :], kv[m2][:, j, hf * 512:hf * 512 + 512], False, True,
                                   reads, t_atri, mark=end)
            kusers.append(m)
            t_hd = tt(dve, tm[:, 0], tm[:, 0], tm[:, 1], ALU.add, reads)
            if late is not None:
                settled(late[0], l0_proj(late[0], *got), t_x)
            late = (i, tm[:, 0], t_hd, tusers)
            if 2 <= i < 2 + len(steps):
                steps[i - 2]()
        got = l0_out(*late)
        settled(late[0], l0_proj(late[0], *got), t_x)
        t_conv = [[(s_, s_.n) for s_ in sv_sem]]

        def moe(l, E, CH, w_rt, b_rt, gated, ready, t_x, t_wd):
            NS = CH * NT + E - 1
            nslab = 3 if gated else 2
            span = 2 * nslab * 2048
            HB = dram(f"HB{l}", [T, 2 * D], f16)
            YT = dram(f"YT{l}", [(CH * NT + NS) * 128, D])
            area = Area(E * span // 2)
            SL = [area(NT) for c in range(CH)]
            GV = [area(NT) for c in range(CH)]
            ei = area(NS).bitcast(i32)
            gi = area(NS).bitcast(i32)
            yi = area(NS).bitcast(i32)
            base = area.at
            l_r = sem(f"l_r{l}")
            RWf = area(2, E)
            RW = area.pair(2, E)
            RB = area(E)
            sp.dma(l_r, RWf, w_rt.rearrange("(k p) n -> p k n", p=128), ready)
            t_r = sp.dma(l_r, RB, b_rt.unsqueeze(0).broadcast_to([128, E]), ready)
            t_rw = split([w.rearrange("p a b -> p (a b)") for w in RW], RWf.rearrange("p a b -> p (a b)"), dve, t_r, ready)
            LG = area(NT, E)
            HR = area.ring(4, D)
            HP = area.ring(3, 2, D, dt=f16)
            HTR = area.ring(2, 4, 128, dt=f16)
            HBv = HB.rearrange("(t p) d -> p t d", p=128)
            everything = now()
            trb = Ring([ps[6], ps[7]])
            trb.free = [list(everything) for _ in range(2)]
            scb = Ring([ps[4], ps[5]])
            scb.free = [list(everything) for _ in range(2)]
            lgp = bank(0, NT, E)
            l_hb = [sem(f"l_hb{l}_{i}") for i in range(3)]
            l_ew = sem(f"l_ew{l}")
            for x in range(E):
                t_w = sp.dma(l_ew, BIG16[:, x * span:(x + 1) * span], WD[l][:, x * span:(x + 1) * span], ready, t_wd)
            def rows_T(src, *after):
                bk, bfree, busers = trb.next()
                b16 = shaped(bk[:, 0:256].bitcast(f16), (4, 128))
                for k in range(4):
                    m = tp16(b16[:, k, :], src[:, k * 128:(k + 1) * 128], *after, bfree, mark=(k == 3))
                return b16, m, busers

            got, t_lg = {}, []

            def h_rows(i):
                b = i // 4
                if i % 4 == 0:
                    sc, sfree, susers = scb.next()
                    got["sc"] = sc, susers, mm(sc[:, :], sel[0:8, b, :], MOD[0:8, l, 3 * D:5 * D], True, True,
                                               t_mod, t_sel, sfree, mark=True)
                sc, susers, t_sc = got["sc"]
                h, hfree, husers = HR.next()
                a = xnorm(h, i, t_x[i // 8], hfree, ready)
                a = tt(dve, h, h, sc[:, 256:512], ALU.mult, a, t_sc)
                a = tt(dve, h, h, sc[:, 0:256], ALU.add, a)
                if i % 4 == 3:
                    susers.append(a)
                got[i] = h, a, husers

            def h_split(i):
                h, a, husers = got[i]
                hp, pfree, pusers = HP.next()
                s_ = split((hp[:, 0, :], hp[:, 1, :]), h, pool, a, pfree)
                husers.extend(s_)
                flat = hp.rearrange("p a b -> p (a b)")
                pusers.append(sp.dma(l_hb[i % 3], HBv[:, i, :], flat, s_))
                got[i] = flat, s_, pusers

            def h_turn(i):
                flat, s_, pusers = got[i]
                b16, m, busers = rows_T(flat, s_)
                pusers.append(m)
                got[i] = b16, m, busers

            def h_copy(i):
                b16, m, busers = got[i]
                ht, tfree, tusers = HTR.next()
                a = copy(act, ht, b16, m, tfree)
                busers.append(a)
                got[i] = ht, a, tusers

            def logits(i):
                ht, a, tusers = got.pop(i)
                for k in range(2):
                    m = mm3(lgp[:, i, :], (ht[:, k, :], ht[:, 2 + k, :]), [w[:, k, :] for w in RW], k == 0, k == 1,
                            a, t_rw, everything, mark=(k == 1))
                tusers.append(m)
                t_lg.append(m)

            pipeline(NT, [h_rows, h_split, h_turn, h_copy, logits])
            m = t_lg[-1]
            t_hb = [(s_, s_.n) for s_ in l_hb]
            cur = tt(dve, LG, lgp, bc(RB, 1, NT), ALU.add, m, t_r)
            late_words = area.at
            MX, W3, PR = area(NT), area(NT, E), area(NT, E)
            AL = area(NT, E, dt=f16)
            OH = [area(NT, E) for _ in range(CH)]
            dec = area(E)
            t_io = iota(dec, [[-1, E]], E, 0, ready)
            if CH == 2:
                cur = dve(lambda e: e.tensor_reduce(MX, LG, AX.X, ALU.max), cur)
                cur = tt(dve, PR, LG, bc(MX, 2, E), ALU.subtract, cur)
                cur = act(lambda e: e.activation(PR, PR, ACT.Exp), cur)
                cur = dve(lambda e: e.tensor_reduce(MX, PR, AX.X, ALU.add), cur)
                cur = dve(lambda e: e.reciprocal(MX, MX), cur)
                cur = tt(dve, PR, PR, bc(MX, 2, E), ALU.mult, cur)
            else:
                cur = act(lambda e: e.activation(PR, LG, ACT.Sigmoid), cur)
            for c in range(CH):
                cur = dve(lambda e, c=c: e.tensor_reduce(GV[c], PR, AX.X, ALU.max), cur)
                cur = tt(dve, W3, PR, bc(GV[c], 2, E), ALU.is_ge, cur)
                cur = tt(dve, W3, W3, bc(dec, 1, NT), ALU.mult, cur, t_io)
                cur = dve(lambda e: e.tensor_reduce(MX, W3, AX.X, ALU.max), cur)
                cur = tt(dve, OH[c], W3, bc(MX, 2, E), ALU.is_equal, cur)
                if c + 1 < CH:
                    cur = dve(lambda e, c=c: e.scalar_tensor_tensor(out=PR, in0=OH[c], scalar=-2.0, in1=PR,
                                                                    op0=ALU.mult, op1=ALU.add), cur)
            if CH == 2:
                cur = tt(dve, MX, GV[0], GV[1], ALU.add, cur)
                cur = dve(lambda e: e.reciprocal(MX, MX), cur)
                for c in range(2):
                    cur = tt(dve, GV[c], GV[c], MX, ALU.mult, cur)
                cur = tt(dve, AL, OH[0], OH[1], ALU.add, cur)
            else:
                cur = copy(dve, AL, OH[0], cur)
            rk, ct = bank(1, NT, E), bank(2, NT, E)
            mm(rk, stri[:, :], AL, True, True, cur, t_stri, t_ones)
            m = mm(ct, ones[:, :], AL, True, True, mark=True)
            CI, zz, cs = area(E, NT), area(NT), area(E, NT)
            cur = dve(lambda e: e.memset(zz, 0.0), m)
            cur = copy(dve, cs, ct.rearrange("p t e -> p e t"), cur)
            for x in range(E):
                t_last = dve(lambda e, x=x: e.tensor_tensor_scan(out=CI[:, x, :], data0=cs[:, x, :], data1=zz, initial=0.0,
                                                                 op0=ALU.add, op1=ALU.add), cur)
            n_i = area(E).bitcast(i32)
            n_p, ends_, bases = area(E), area(E), area(E)
            cur = dve(lambda e: e.tensor_scalar(n_p, CI[:, :, NT - 1], 127.0, None, ALU.add), t_last)
            cur = copy(dve, n_i, n_p, cur)
            cur = dve(lambda e: e.tensor_scalar(n_i, n_i, 7, 7, ALU.arith_shift_right, ALU.arith_shift_left), cur)
            cur = copy(dve, n_p, n_i, cur)
            cur = dve(lambda e: e.tensor_tensor_scan(out=ends_, data0=n_p, data1=zz[:, 0:E], initial=0.0,
                                                     op0=ALU.add, op1=ALU.add), cur)
            cur = tt(dve, bases, ends_, n_p, ALU.subtract, cur)
            cur = tt(dve, CI, CI, cs, ALU.subtract, cur)
            cur = tt(dve, CI, CI, bc(bases, 2, NT), ALU.add, cur)
            PS_ = area(NT, E)
            cur = tt(dve, PS_, rk, CI.rearrange("p e t -> p t e"), ALU.add, cur)
            for c in range(CH):
                cur = tt(dve, W3, PS_, OH[c], ALU.mult, cur)
                cur = dve(lambda e, c=c: e.tensor_reduce(SL[c], W3, AX.X, ALU.add), cur)
            it = area(NS)
            ex = area(NS)
            it128 = area(NS)
            t_it = iota(it, [[1, NS]], 0, 0, ready)
            t_it = iota(it128, [[128, NS]], 0, 0, ready)
            lap = Area(base) if l else area
            if l:
                dve.wait(now(pe, act, pool), t_hb)
            cmp_ = lap(NS, E)
            cur = tt(dve, cmp_, bc(ends_, 1, NS), bc(it128, 2, E), ALU.is_le, cur, t_it)
            cur = dve(lambda e: e.tensor_reduce(ex, cmp_, AX.X, ALU.add), cur)
            cur = dve(lambda e: e.tensor_scalar(ex, ex, float(E - 1), float(span), ALU.min, ALU.mult), cur)
            t_ei = copy(dve, ei, ex, cur)
            s_i, s_lo, s_hi = area(NT).bitcast(i32), area(NT), area(NT)
            s_j = area(NT).bitcast(i32)
            G = 8
            S1 = lap.ring(2, G, 128, dt=f16)
            A1 = lap.ring(2, G, 2, NS, dt=f16)
            assert not l or lap.at <= late_words
            mp = bank(3, 2, NS)
            cur = t_ei
            for c in range(CH):
                cur = copy(dve, s_i, SL[c], cur)
                cur = dve(lambda e: e.tensor_scalar(s_j, s_i, 7, None, ALU.arith_shift_right), cur)
                cur = copy(dve, s_hi, s_j, cur)
                cur = dve(lambda e, c=c: e.scalar_tensor_tensor(out=s_lo, in0=s_hi, scalar=-128.0, in1=SL[c],
                                                                op0=ALU.mult, op1=ALU.add), cur)
                for g in range(0, NT, G):
                    s1, sfree, susers = S1.next()
                    a1, afree, ausers = A1.next()
                    u = tt(dve, s1, bc(s_lo[:, g:g + G], 2, 128), bc(iota_p[:, :], 1, G), ALU.is_equal, cur, sfree, t_iota)
                    v = tt(dve, a1[:, :, 0, :], bc(s_hi[:, g:g + G], 2, NS), bc(it, 1, G), ALU.is_equal, cur, afree)
                    w = dve(lambda e, a1=a1: e.tensor_scalar(a1[:, :, 1, :], a1[:, :, 0, :], pcol[:, 0:1], None, ALU.mult), v)
                    v = tt(dve, a1[:, :, 0, :], a1[:, :, 0, :], bc(tile_no[:, c, g:g + G], 2, NS), ALU.mult, w)
                    for n in range(G):
                        m = mm(mp, s1[:, n, :], a1[:, n, :, :], c == 0 and g == 0 and n == 0, c == CH - 1 and g == NT - G and n == G - 1,
                               u, v, everything, mark=(n == G - 1))
                    susers.append(m)
                    ausers.append(m)
                    cur = v
            rf, pad = area(NS), area(NS)
            slot_no = area(NS)
            t_sn = iota(slot_no, [[128, NS]], CH * NT * 128, 1, ready)
            r_i = area(NS).bitcast(i32)
            cur = dve(lambda e: e.tensor_scalar(pad, mp[:, 0, :], 1.0, None, ALU.is_lt), m)
            cur = dve(lambda e: e.tensor_scalar(rf, mp[:, 0, :], 128.0, -128.0, ALU.mult, ALU.add), cur)
            cur = tt(dve, rf, rf, mp[:, 1, :], ALU.add, cur)
            cur = copy(dve, r_i, rf, cur)
            t_gi = dve(lambda e: e.tensor_scalar(gi, r_i, T - 1, None, ALU.bitwise_and), cur)
            cur = tt(dve, slot_no, slot_no, rf, ALU.subtract, cur, t_sn)
            cur = tt(dve, slot_no, slot_no, pad, ALU.mult, cur)
            cur = tt(dve, rf, rf, slot_no, ALU.add, cur)
            t_yi = copy(dve, yi, rf, cur)

            area = Area(base)
            HIN = area.ring(3, 2 * D, dt=f16)
            HTT = area.ring(2, 4, 128, dt=f16)
            UP = area.ring(2, 1024)
            UPT = area.pairs(1 if l else 2, 8, 128)
            YO = area.ring(2, D)
            if l == 0:
                st_, hv_ = area.ring(2, 1024), area.pairs(2, 1024)
            everything = now()
            for q in (act, dve, pe, pool, sp):
                q.wait(everything, t_hb)
            wide = Ring([ps[0], ps[1], ps[2], ps[3]])
            trb = Ring([ps[6], ps[7]])
            yb = Ring([ps[4], ps[5]])
            l_hi = [sem(f"l_hi{l}_{i}") for i in range(3)]
            l_yo = [sem(f"l_yo{l}_{i}") for i in range(2)]
            regs = {}

            def reg(j):
                def f(e):
                    regs.pop(j - 3, None)
                    regs[j] = e.value_load(ei[0:1, j:j + 1], min_val=0, max_val=(E - 1) * span)
                pe.wait(t_ei, t_w)
                pe.items.append(f)

            def mm_w(out, lhs, j, at, n, start, stop, *after, mark=False):
                for p, (m, w) in enumerate(((0, 0), (0, 1), (1, 0))):
                    r = pe(lambda e, m=m, w=w, p=p: e.matmul(
                        out, lhs[m], BIG16[:, bass.ds(regs[j] + (w * nslab * 2048 + at), n)],
                        start=start and p == 0, stop=stop and p == 2, skip_group_check=True),
                        *after, mark=mark and p == 2)
                return r

            def fetch(j):
                h, hfree, husers = HIN.next()
                return h, pool.gather(l_hi[j % 3], h, HB, gi[:, j:j + 1], t_gi, t_hb, hfree), husers

            def turn(j, h, a, husers):
                b16, m, busers = rows_T2(h, a)
                husers.append(m)
                ht, tfree, tusers = HTT.next()
                a = copy(act, ht, b16, m, tfree)
                busers.append(a)
                return ht, a, tusers

            def rows_T2(src, *after):
                bk, bfree, busers = trb.next()
                b16 = shaped(bk[:, 0:256].bitcast(f16), (4, 128))
                for k in range(4):
                    m = tp16(b16[:, k, :], src[:, k * 128:(k + 1) * 128], *after, bfree, mark=(k == 3))
                return b16, m, busers

            def up(j, hf, ht, a, u, ufree):
                bks = []
                for w in range(2 if gated else 1):
                    bk, bfree, busers = wide.next()
                    for k in range(2):
                        m = mm_w(bk[:, :], (ht[:, k, :], ht[:, 2 + k, :]), j, 2048 * w + 1024 * k + 512 * hf, 512,
                                 k == 0, k == 1, a, bfree, mark=(k == 1))
                    bks.append((bk, m, busers))
                us = u[:, hf * 512:hf * 512 + 512]
                bk, m, busers = bks[0]
                s_ = act(lambda e: e.activation(us, bk[:, :], ACT.Silu if gated else ACT.Gelu), m, ufree)
                busers.append(s_)
                if gated:
                    bk2, m2, busers2 = bks[1]
                    s_ = tt(dve, us, us, bk2[:, :], ALU.mult, s_, m2)
                    busers2.append(s_)
                return s_, bks[-1][1]

            def u_T(u, parts, uusers):
                ut, tfree, tusers = UPT.next()
                cp = []
                for q in range(2):
                    bk, bfree, busers = trb.next()
                    for n in range(4):
                        m = tp(bk[:, n * 128:(n + 1) * 128], u[:, (4 * q + n) * 128:(4 * q + n + 1) * 128],
                               parts[q], bfree, mark=(n == 3))
                    uusers.append(m)
                    s_ = split([h[:, 4 * q:4 * q + 4, :] for h in ut], bk[:, :].rearrange("p (j n) -> p j n", j=4),
                               dve, m, tfree)
                    busers.extend(s_)
                    cp.append(s_)
                return ut, cp, tusers

            def down(j, ut, cp, tusers):
                bk, bfree, busers = yb.next()
                for n in range(8):
                    m = mm_w(bk[:, 0:256], [h[:, n, :] for h in ut], j, (nslab - 1) * 2048 + 256 * n, 256, n == 0, n == 7,
                             cp[n // 4], bfree, mark=(n == 7))
                tusers.append(m)
                y, yfree, yusers = YO.next()
                a = copy(act, y, bk[:, 0:256], m, yfree)
                busers.append(a)
                yusers.append(pool.scatter(l_yo[j % 2], YT, yi[:, j:j + 1], y, a, t_yi))

            fetched = [fetch(0), fetch(1)]
            turned = turn(0, *fetched[0])
            reg(0)
            late = None
            if l == 0:
                steps = converter(1, st_, hv_, pool)
            for j in range(NS):
                ht, t_ht, tusers = turned
                if j + 1 < NS:
                    reg(j + 1)
                u, ufree, uusers = UP.next()
                p0, _ = up(j, 0, ht, t_ht, u, ufree)
                if late:
                    got = u_T(*late)
                p1, m = up(j, 1, ht, t_ht, u, ufree)
                tusers.append(m)
                if j + 2 < NS:
                    fetched.append(fetch(j + 2))
                if j + 1 < NS:
                    turned = turn(j + 1, *fetched[j + 1])
                if late:
                    down(j - 1, *got)
                late = (u, (p0, p1), uusers)
                if l == 0 and j % 2 == 0 and j // 2 < len(steps):
                    steps[j // 2]()
            got = u_T(*late)
            down(NS - 1, *got)
            t_ys = [(s_, s_.n) for s_ in l_yo]
            area = Area(base)
            YI = area.ring(3, CH, 4, D)
            l_yi = [sem(f"l_yi{l}_{i}") for i in range(3)]
            gb = Ring([ps[0], ps[1], ps[2]])
            everything = now()
            outs = []
            YTv = YT[0:CH * T, :].rearrange("(c t p) d -> p c t d", c=CH, p=128)
            got = {}

            def rows_in(g):
                gk, gfree, gusers = gb.next()
                t_g = gates(l, 1, gk, g, gfree, everything)
                y4, yfree, yusers = YI.next()
                for c in range(CH):
                    t_y4 = sp.dma(l_yi[g % 3], y4[:, c], YTv[:, c, 4 * g:4 * g + 4, :], t_ys, yfree, everything)
                got[g] = gk, t_g, gusers, y4, t_y4, yusers

            def combine(i):
                gk, t_g, gusers, y4, t_y4, yusers = got[i // 4]
                y = y4[:, 0, i % 4, :]
                a = act(lambda e: e.activation(y, y, ACT.Copy, scale=GV[0][:, i:i + 1]), t_y4)
                if CH == 2:
                    y2 = y4[:, 1, i % 4, :]
                    a = dve(lambda e: e.scalar_tensor_tensor(
                        out=y, in0=y2, scalar=GV[1][:, i:i + 1], in1=y, op0=ALU.mult, op1=ALU.add), a)
                a = tt(dve, y, y, gk[:, 0:256], ALU.mult, a, t_g)
                if i % 4 == 3:
                    gusers.append(a)
                a = tt(pool if l == 0 else dve, X[:, i, :], X[:, i, :], y, ALU.add, a)
                got[i + 100] = a
                if i % 4 == 3:
                    yusers.append(a)
                if l:
                    finished(i, a)

            def stats_in(i):
                if l == 0:
                    settled(i, got.pop(i + 100), outs)

            for g in range(3):
                rows_in(g)
            for i in range(NT + 1):
                if i < NT:
                    combine(i)
                if i % 4 == 3 and i // 4 + 3 < NT // 4:
                    rows_in(i // 4 + 3)
                if i:
                    stats_in(i - 1)
            return outs

        l_o = sem("l_o")
        ov = out.rearrange("(t p) d -> p t d", p=128)

        def finished(i, a):
            if i % 4 == 3:
                sp.dma(l_o, ov[:, i - 3:i + 1, :], X[:, i - 3:i + 1, :], a)

        if phases >= 2:
            before = now()
            phase_sems(1)
            t_x = moe(0, 4, 2, rw_in, rb_in, True, before, t_x, t_conv)
            t_conv = [[(s_, s_.n) for s_ in sv_sem]]

        if phases >= 3:
            before = now()
            phase_sems(2)
            area = Area(0)
            HFh, HFl = area.pair(2, 2048)
            QK = area.ring(2, 16, 256)
            PB = area.ring(3, 2, 16, 64)
            PV = area.ring(1, 2, 1024)
            ET = area.ring(2, 16, 16, 16)
            DF = area.ring(2, 2, 16, 16)
            SM = area.ring(4, 2, 16)
            RS = area.ring(1, 16, 16)
            OB = area.ring(2, 16, 64)
            Wq, Wu = area.pair(2, 1024), area.pair(2, 256)
            wst = PB.bufs[0].rearrange('p q k f -> p (q k f)').rearrange('p (a b) -> p a b', a=2)
            wsu = PB.bufs[1].rearrange('p q k f -> p (q k f)')[:, 0:512].rearrange('p (a b) -> p a b', a=2)
            xnr, vr1 = area.ring(3, D), area.ring(2, 2, 128)
            l_w1 = sem("l_w1")
            sp.dma(l_w1, wst, qkvw_in.rearrange("(k p) n -> p k n", p=128), before)
            t_w1 = sp.dma(l_w1, wsu, wout_in.rearrange("(k p) n -> p k n", p=128), before)
            for q in (dve, act, pool, pe):
                q.wait(before)
            flat = "p a b -> p (a b)"
            t_wq = split([w.rearrange(flat) for w in Wq], wst.rearrange(flat), pool, t_w1)
            t_wq += split([w.rearrange(flat) for w in Wu], wsu.rearrange(flat), pool, t_w1)
            OW = dram("OW", [T * 4, 64])
            tr = Ring([ps[6], ps[7]])
            qb = Ring([ps[0], ps[1]])
            sb_ = Ring([ps[2], ps[3], ps[4]])
            eb = Ring([ps[5]])
            l_ow = [sem(f"l_ow{i}") for i in range(2)]

            def place(n, v):
                h0, b = 4 * (n // 4), n % 4

                def at(h_):
                    return h_.rearrange("p k (h b t) -> p k h b t", h=16, b=4)[:, :, h0:h0 + 4, b, :]
                return at(HFh), at(HFl), v.rearrange("p k (h t) -> p k h t", h=4)

            t_read = [None] * 16

            def norms(bh):
                ends = []
                tiles = [16 * bh + 4 * (n % 4) + n // 4 for n in range(16)]
                return ends, norm_T(1, place, (xnr, vr1), tr, lambda i: t_x[i // 8], tiles, ends)

            def project(buf, h, ci, t_h):
                qk, free, t_cp = buf
                bk, bfree, busers = qb.next()
                for k in range(2):
                    m = mm3(bk[:, 0:256], (HFh[:, k, 128 * h:128 * h + 128], HFl[:, k, 128 * h:128 * h + 128]),
                            [w[:, k, 256 * ci:256 * ci + 256] for w in Wq], k == 0, k == 1,
                            t_h, bfree, t_wq, mark=(k == 1))
                a = copy(act, qk[:, h, :], bk[:, 0:256], m, free)
                busers.append(a)
                t_cp.append(a)
                t_read[h] = m

            def scores(qk, t_cp, q2):
                pb, pfree, pusers = PB.next()
                ms = []
                for q in range(2):
                    ms.append(tt(pool, pb[:, q], bc(qk[:, 2 * q2 + q, 0:64], 1, 16), qk[:, :, 64:128], ALU.mult,
                                 t_cp, pfree, t_wq))
                bk, bfree, busers = sb_.next()
                pv = pb.rearrange("p q k (f d) -> p (q k f) d", d=4)
                for d in range(4):
                    m = mm(bk[:, :], ident[:, :], pv[:, :, d], d == 0, d == 3, ms, bfree, mark=(d == 3))
                pusers.append(m)
                return bk, m, busers

            def soft(et, efree, q2, bk, m, busers):
                s4 = bk[:, :].rearrange("p (q k f) -> p q k f", q=2, k=16)
                sm, sfree, susers = SM.next()
                df, dfree, dusers = DF.next()
                a = dve(lambda e: e.tensor_reduce(sm, s4.rearrange("p q k f -> p q f k"), AX.X, ALU.max), m, sfree)
                a = tt(dve, df, s4, bc(sm, 2, 16), ALU.subtract, a, dfree)
                busers.append(a)
                susers.append(a)
                a = act(lambda e: e.activation(et[:, :, 2 * q2:2 * q2 + 2, :].rearrange("p k q f -> p q k f"), df,
                                               ACT.Exp, scale=0.5), a, efree)
                dusers.append(a)
                return a

            def values(qk, q2, ob, ofree, et, a):
                pv, pfree, pusers = PV.next()
                ms = []
                for q in range(2):
                    ms.append(tt(dve, pv[:, q].rearrange("p (f d k) -> p f d k", f=16, d=4),
                                 bc(et[:, :, 2 * q2 + q, :].rearrange("p k f -> p f k"), 2, 4),
                                 qk[:, :, 128:192].rearrange("p k (f d) -> p f d k", d=4), ALU.mult, a, pfree))
                o2 = ob[:, 2 * q2:2 * q2 + 2, :]
                r = dve(lambda e: e.tensor_reduce(o2, pv.rearrange("p q (n k) -> p (q n) k", k=16), AX.X, ALU.add), ms, ofree)
                pusers.append(r)
                return r, ms[-1]

            def totals(et, a):
                bk, bfree, busers = eb.next()
                for k in range(16):
                    m = mm(bk[:, 0:256], ident[:, :], et[:, k].rearrange("p q f -> p (q f)"), k == 0, k == 15,
                           a, bfree, mark=(k == 15))
                return bk, m, busers

            def finish(c, qk, qusers, ob, ousers, r, bk, m, busers):
                bh, ci = c // 4, c % 4
                rs, rfree, rusers = RS.next()
                a = dve(lambda e: e.reciprocal(rs.rearrange("p q f -> p (q f)"), bk[:, 0:256]), m, rfree)
                busers.append(a)
                a = tt(dve, rs4(ob), rs4(ob), bc(rs, 3, 4), ALU.mult, a, r)
                rusers.append(a)
                a = tt(dve, ob, ob, qk[:, :, 192:256], ALU.mult, a)
                qusers.append(a)
                for b in range(4):
                    r0 = (ci * 8 + bh * 4 + b) * 512
                    ousers.append(sp.dma(l_ow[c % 2], OW[r0:r0 + 512, :].rearrange("(h t) f -> t h f", t=32),
                                         ob[32 * b:32 * b + 32, :, :], a))

            def rs4(ob):
                return ob.rearrange("p q (f d) -> p q f d", d=4)

            ends, stages = norms(0)
            bufs = [(*QK.next(), )]
            bufs[0] = (bufs[0][0], bufs[0][1], [], bufs[0][2])
            pipeline(16, stages + [lambda n: [project(bufs[0][:3], h, 0, ends[0:n + 1]) for h in range(n - 3, n + 1)]
                                   if n % 4 == 3 else None])
            chunk, sc, sf = {}, {}, {}
            N = 64

            def do_scores(s_):
                if s_ < N:
                    qk, free, t_cp, qusers = bufs[s_ // 8]
                    sc[s_] = scores(qk, t_cp, s_ % 8)

            def do_soft(s_):
                if s_ < N:
                    if s_ % 8 == 0:
                        chunk[s_ // 8] = ET.next()
                    et, efree, eusers = chunk[s_ // 8]
                    sf[s_] = soft(et, efree, s_ % 8, *sc.pop(s_))
            do_scores(0)
            do_scores(1)
            do_soft(0)
            pend = None
            for s_ in range(N):
                c, q2 = s_ // 8, s_ % 8
                qk, free, t_cp, qusers = bufs[c]
                et, efree, eusers = chunk[c]
                if q2 == 0:
                    ob, ofree, ousers = OB.next()
                if c < 7:
                    if c == 3 and q2 < 4:
                        if q2 == 0:
                            ends, stages = norms(1)
                            stages[3] = (lambda f: lambda n: (act.wait(t_read[4 * (n // 4):4 * (n // 4) + 4]), f(n)))(stages[3])
                        pipeline(16, stages, 4 * q2, 4 * q2 + 4 if q2 < 3 else None)
                    if q2 == 2:
                        nq, nfree, nusers = QK.next()
                        bufs.append((nq, nfree, [], nusers))
                    if 2 <= q2 < 6:
                        for h in range(4 * (q2 - 2), 4 * (q2 - 2) + 4):
                            project(bufs[c + 1][:3], h, (c + 1) % 4, ends[0:4 * (h // 4) + 4])
                do_scores(s_ + 2)
                do_soft(s_ + 1)
                r, last = values(qk, q2, ob, ofree, et, sf[s_])
                if q2 == 7:
                    tot = totals(et, [sf[8 * c + n] for n in range(8)])
                    eusers.extend([last, tot[1]])
                    pend = (c, qk, qusers, ob, ousers, r, *tot)
                if q2 == 1 and pend:
                    finish(*pend)
                    pend = None
            finish(*pend)
            t_ow = [(s_, s_.n) for s_ in l_ow]
            everything = now()
            area = Area(0)
            OI, OIP, OIT, YG = area.ring(4, D), area.ring(2, 2, D, dt=f16), area.ring(2, 4, 128, dt=f16), area.ring(2, D)
            for q in (dve, act, pool, pe, sp):
                q.wait(everything)
            OWv = OW.rearrange("(t p r) f -> t p (r f)", p=128, r=4)
            l_oi = [sem(f"l_oi{i}") for i in range(4)]
            gb = Ring([ps[2], ps[3]])
            GS = area.ring(2, D)
            t_x2 = []
            got = {}

            def w_load(i):
                oi, free, users = OI.next()
                got[i] = oi, sp.dma(l_oi[i % 4], oi, OWv[i], t_ow, free), users

            def w_split(i):
                oi, a, users = got[i]
                op_, pfree, pusers = OIP.next()
                s_ = split((op_[:, 0, :], op_[:, 1, :]), oi, pool, a, pfree)
                users.extend(s_)
                got[i] = op_.rearrange("p a b -> p (a b)"), s_, pusers

            def w_turn(i):
                fl, s_, pusers = got[i]
                bk, bfree, busers = tr.next()
                b16 = shaped(bk[:, 0:256].bitcast(f16), (4, 128))
                for k in range(4):
                    m = tp16(b16[:, k, :], fl[:, k * 128:(k + 1) * 128], s_, bfree, mark=(k == 3))
                pusers.append(m)
                got[i] = b16, m, busers

            def w_copy(i):
                b16, m, busers = got[i]
                ot, tfree, tusers = OIT.next()
                a = copy(act, ot, b16, m, tfree)
                busers.append(a)
                got[i] = ot, a, tusers

            def w_product(i):
                if i % 4 == 0:
                    gk, gfree, gusers = gb.next()
                    gs, sfree, susers = GS.next()
                    a = copy(act, gs, gk[:, 0:256], gates(1, 0, gk, i // 4, gfree), sfree)
                    gusers.append(a)
                    got["g"] = gs, susers, a
                ot, a, tusers = got[i]
                bk, bfree, busers = qb.next()
                for k in range(2):
                    m = mm3(bk[:, 0:256], (ot[:, k, :], ot[:, 2 + k, :]), [w[:, k, :] for w in Wu], k == 0, k == 1,
                            a, bfree, mark=(k == 1))
                tusers.append(m)
                got[i] = bk, m, busers, got["g"]

            def w_add(i):
                bk, m, busers, (gs, susers, t_g) = got.pop(i)
                yg, yfree, yusers = YG.next()
                y = tt(dve, yg, bk[:, 0:256], gs, ALU.mult, m, yfree, t_g)
                busers.append(y)
                if i % 4 == 3:
                    susers.append(y)
                y = tt(dve, X[:, i, :], X[:, i, :], yg, ALU.add, y)
                yusers.append(y)
                settled(i, y, t_x2)

            pipeline(NT, [w_load, lambda i: None, w_split, w_turn, w_copy, w_product, w_add])
            t_x = t_x2

        if phases >= 4:
            before = now()
            phase_sems(3)
            t_x = moe(1, 8, 1, wr_in, br_in, False, before, t_x, t_conv)

        if phases < 4:
            for i in range(3, NT, 4):
                finished(i, now())
        sp.wait((l_o, l_o.n))

        block = ctx.enter_context(nc.Block())
        block.sync(sp.play)
        block.gpsimd(pool.play)
        block.scalar(act.play)
        block.vector(dve.play)
        block.tensor(pe.play)


def lay_out(i, np):
    a = {k: np.ascontiguousarray(v) for k, v in i.items()}
    return {
        "x": a["L0_attn_query"].reshape(T, D),
        "wqk": np.ascontiguousarray(np.concatenate([a["L0_attn_W_Q"][:, :, 0], a["L0_attn_W_K"][:, :, 0]]).T),
        "wv": np.ascontiguousarray(a["L0_attn_W_V"].transpose(1, 0, 2).reshape(D, 1024)),
        "wo": np.ascontiguousarray(a["L0_attn_W_O"].transpose(2, 1, 0).reshape(1024, D)),
        "rw": a["L0_ffn_router_w"], "rb": a["L0_ffn_router_b"],
        "w1": a["L0_ffn_w1"], "w3": a["L0_ffn_w3"], "w2": a["L0_ffn_w2"],
        "c0": a["L0_c"], "m0": a["L0_wmod"],
        "qkvw": a["L1_attn_w_qkvw"], "wout": a["L1_attn_w_out"],
        "wr": a["L1_ffn_Wr"], "br": a["L1_ffn_br"], "v1": a["L1_ffn_W1"], "v2": a["L1_ffn_W2"],
        "c1": a["L1_c"], "m1": a["L1_wmod"],
    }


def kernel(**inputs):
    import numpy as np
    import concourse.bacc as bacc
    from concourse.bass_utils import run_bass_kernel_spmd

    nc = bacc.Bacc("TRN2", target_bir_lowering=False, num_devices=1)
    arrays = {f"in_{k}": v for k, v in lay_out(inputs, np).items()}
    args = [nc.dram_tensor(k, v.shape, mybir.dt.from_np(v.dtype), kind="ExternalInput").ap() for k, v in arrays.items()]
    out = nc.dram_tensor("out_0", (T, D), fp32, kind="ExternalOutput").ap()
    program(nc, *args, out)
    r = run_bass_kernel_spmd(nc, [arrays], core_ids=[0])
    return r.results[0]["out_0"].reshape(B, S, D)
```

```python
import math

import concourse.bass as bass
from concourse import mybir

fp32 = mybir.dt.float32
i32 = mybir.dt.int32
f16 = mybir.dt.float16
ALU = mybir.AluOpType
ACT = mybir.ActivationFunctionType
AX = mybir.AxisListType

B, S, D = 8, 512, 256
T = B * S
NT = T // 128
PI = math.pi
BIGW = 39680


class Sem:

    def __init__(self, sem):
        self.sem, self.n = sem, 0

    def up(self, by):
        self.n += by
        return (self, self.n)


class Queue:

    def __init__(self, name):
        self.name, self.items, self.done, self.seen = name, [], None, {}

    def wait(self, *tokens):
        most = {}

        def collect(ts):
            for t in ts:
                if isinstance(t, list):
                    collect(t)
                elif t is not None:
                    most[t[0]] = max(most.get(t[0], 0), t[1])
        collect(tokens)
        for sem, n in most.items():
            if self.seen.get(sem, 0) < n:
                self.seen[sem] = n
                self.items.append(lambda e, s=sem.sem, n=n: e.wait_ge(s, n))

    def __call__(self, f, *after, mark=True):
        self.wait(*after)
        if not mark:
            self.items.append(f)
            return None
        t = self.done.up(1)
        self.items.append(lambda e, f=f, s=t[0].sem: f(e).then_inc(s, 1))
        return t

    def dma(self, sem, out, in_, *after):
        self.wait(*after)
        t = sem.up(16)
        self.items.append(lambda e: e.dma_start(out, in_).then_inc(sem.sem, 16))
        return t

    def scatter(self, sem, out, idx, in_, *after):
        self.wait(*after)
        t = sem.up(16)
        self.items.append(lambda e: e.indirect_dma_start(
            out, bass.IndirectOffsetOnAxis(idx, 0), in_, None).then_inc(sem.sem, 16))
        return t

    def gather(self, sem, out, in_, idx, *after):
        self.wait(*after)
        t = sem.up(16)
        self.items.append(lambda e: e.indirect_dma_start(
            out, None, in_, bass.IndirectOffsetOnAxis(idx, 0)).then_inc(sem.sem, 16))
        return t

    def play(self, e):
        for f in self.items:
            f(e)


class Ring:

    def __init__(self, bufs):
        self.bufs, self.free, self.i = bufs, [[] for _ in bufs], -1

    def next(self):
        self.i = (self.i + 1) % len(self.bufs)
        free, self.free[self.i] = self.free[self.i], []
        return self.bufs[self.i], free, self.free[self.i]


def program(nc, x_in, wqk_in, wv_in, wo_in, rw_in, rb_in, w1_in, w3_in, w2_in, c0_in, m0_in,
            qkvw_in, wout_in, wr_in, br_in, v1_in, v2_in, c1_in, m1_in, out):
    from contextlib import ExitStack
    ctx = ExitStack()
    with ctx:
        def sb(name, shape, dt=fp32):
            return ctx.enter_context(nc.sbuf_tensor(name, shape, dt))

        def sem(name):
            return Sem(ctx.enter_context(nc.semaphore(name)))

        X = sb("X", [128, NT, D])
        BIG = sb("BIG", [128, BIGW])
        BIG16 = BIG[:, :].bitcast(f16)
        ident = sb("ident", [128, 128])
        ident16 = sb("ident16", [128, 128], f16)
        tri = sb("tri", [128, 128], f16)
        atri = sb("atri", [128, 128], f16)
        stri = sb("stri", [128, 128], f16)
        ones = sb("ones", [128, 128], f16)
        sel = sb("sel", [8, 8, 128])
        MOD = sb("MOD", [8, 2, 6 * D])
        modT = sb("modT", [128, 2, 4, 8])
        stat = sb("stat", [128, NT, 2])
        rstd = sb("rstd", [128, NT])
        half_pi = sb("half_pi", [128, 1])
        bnst = sb("bnst", [128, 4, 6])
        pcol = sb("pcol", [128, 1])
        iota_p = sb("iota_p", [128, 128])
        tile_no = sb("tile_no", [128, 2, NT])

        ps = [ctx.enter_context(nc.psum_tensor(f"ps{i}", [128, 512], fp32)) for i in range(8)]

        def dram(name, shape, dt=fp32):
            return nc.dram_tensor(name, shape, dt, kind="Internal").ap()

        def shaped(v, shape):
            if len(shape) == 1:
                return v
            names = "abcdef"[:len(shape)]
            return v.rearrange(f"p ({' '.join(names)}) -> p {' '.join(names)}",
                               **{k: s for k, s in zip(names[1:], shape[1:])})

        def view(off, *shape, dt=None, parts=128):
            n = math.prod(shape)
            words = n // 2 if dt == f16 else n
            assert off + words <= BIGW, (off, shape)
            v = BIG[0:parts, off:off + words]
            return shaped(v.bitcast(dt) if dt is not None else v, shape)

        class Area:

            def __init__(self, start):
                self.at = start

            def __call__(self, *shape, dt=None, parts=128):
                v = view(self.at, *shape, dt=dt, parts=parts)
                n = math.prod(shape)
                self.at += (n + 1) // 2 if dt == f16 else n
                return v

            def ring(self, n, *shape, dt=None):
                return Ring([self(*shape, dt=dt) for _ in range(n)])

            def pair(self, *shape):
                return self(*shape, dt=f16), self(*shape, dt=f16)

            def pairs(self, n, *shape):
                return Ring([self.pair(*shape) for _ in range(n)])

        pe, dve, act, pool, sp = (Queue(n) for n in ("pe", "dve", "act", "pool", "sp"))

        def phase_sems(n):
            for q in (pe, dve, act, pool):
                q.done = sem(f"{q.name}_{n}")

        def now(*queues):
            return [(q.done, q.done.n) for q in (queues or (pe, dve, act, pool)) if q.done.n]

        def mm(out, lhsT, rhs, start, stop, *after, mark=False):
            return pe(lambda e: e.matmul(out, lhsT, rhs, start=start, stop=stop, skip_group_check=True),
                      *after, mark=mark)

        def mm3(out, lhs, rhs, start, stop, *after, mark=False):
            mm(out, lhs[0], rhs[0], start, False, *after)
            mm(out, lhs[0], rhs[1], False, False)
            return mm(out, lhs[1], rhs[0], False, stop, mark=mark)

        def tp(out, in_, *after, mark=False, n=128):
            return pe(lambda e: e.transpose(out, in_, ident[0:n, 0:n]), *after, mark=mark)

        def tp16(out, in_, *after, mark=False):
            return pe(lambda e: e.transpose(out, in_, ident16[:, :]), *after, mark=mark)

        def copy(q, out, in_, *after):
            if q is act:
                return act(lambda e: e.activation(out, in_, ACT.Copy), *after)
            return q(lambda e: e.tensor_copy(out, in_), *after)

        def tt(q, out, a, b, op, *after):
            return q(lambda e: e.tensor_tensor(out, a, b, op), *after)

        def split(pair, src, q_lo, *after):
            h = copy(act, pair[0], src, *after)
            return [h, tt(q_lo, pair[1], src, pair[0], ALU.subtract, h)]

        def bank(i, *shape, dt=None):
            n = math.prod(shape)
            if dt == f16:
                return shaped(ps[i][:, 0:n // 2].bitcast(f16), shape)
            return shaped(ps[i][:, 0:n], shape)

        def bc(ap, axis, n):
            a = ap.unsqueeze(axis)
            shape = list(a.shape)
            shape[axis] = n
            return a.broadcast_to(shape)

        def pipeline(n, stages, begin=0, end=None):
            steps = n + len(stages) - 1
            for t in range(begin, steps if end is None else min(end, steps)):
                for s in reversed(range(len(stages))):
                    if 0 <= t - s < n:
                        stages[s](t - s)

        phase_sems(0)

        l_x = [sem(f"l_x{i}") for i in range(4)]
        xt = []
        xv = x_in.rearrange("(t p) d -> p t d", p=128)
        l_c = sem("l_c")
        area = Area(22912)
        WM = area(2, 2, 6 * D)
        CS = area(2, D, parts=8)
        cT = area(2, 2, 8)
        GT = area(2, 2, D, parts=8)
        mod_end = area.at
        wst = area(4160)
        l_m = [sem(f"l_m{l}") for l in range(2)]
        l_w = sem("l_w")

        def load_x(i):
            xt.append(sp.dma(l_x[i], X[:, 8 * i:8 * i + 8, :], xv[:, 8 * i:8 * i + 8, :]))
        sp.dma(l_c, CS[:, 0, :], c0_in)
        t_c = sp.dma(l_c, CS[:, 1, :], c1_in)
        load_x(0)
        t_wm = [sp.dma(l_m[0], WM[:, 0], m0_in.rearrange("(k p) n -> p k n", p=128))]
        load_x(1)
        sp.dma(l_w, shaped(wst[:, 0:64], (2, 32)), wqk_in.rearrange("(k p) n -> p k n", p=128))
        sp.dma(l_w, shaped(wst[:, 64:2112], (2, 1024)), wv_in.rearrange("(k p) n -> p k n", p=128))
        t_lw = sp.dma(l_w, shaped(wst[:, 2112:4160], (8, 256)), wo_in.rearrange("(k p) n -> p k n", p=128))
        load_x(2)
        load_x(3)
        t_wm.append(sp.dma(l_m[1], WM[:, 1], m1_in.rearrange("(k p) n -> p k n", p=128)))

        t = [pool(lambda e, a=a, v=v: e.memset(a, v)) for a, v in
             ((ident[:, :], 0.0), (tri[:, :], 1.0), (stri[:, :], 1.0), (atri[:, :], 1.0),
              (ones[:, :], 1.0), (sel[:, :, :], 0.0), (half_pi[:, :], PI / 2))]

        def affine(ap, cmp, fill, base, pattern, cm, *after):
            return pool(lambda e: e.affine_select(out=ap, in_=ap, compare_op=cmp, fill=fill, base=base,
                                                  pattern=pattern, channel_multiplier=cm), *after)

        def iota(ap, pattern, base=0, cm=0, *after):
            return pool(lambda e: e.iota(ap, pattern, base=base, channel_multiplier=cm,
                                         allow_small_or_imprecise_dtypes=True), *after)
        t_id = affine(ident[:, :], ALU.not_equal, 1.0, 0, [[-1, 128]], 1, t[0])
        t_tri = affine(tri[:, :], ALU.is_ge, 0.0, 0, [[1, 128]], -1, t[1])
        t_stri = affine(stri[:, :], ALU.is_ge, 0.0, -1, [[1, 128]], -1, t[2])
        t_atri = affine(atri[:, :], ALU.is_ge, 0.0, -1, [[-1, 128]], 1, t[3])
        t_sel = affine(sel[:, :, :], ALU.not_equal, 1.0, 0, [[-1, 8], [0, 128]], 1, t[5])
        t_id16 = copy(pool, ident16[:, :], ident[:, :], t_id)
        iota(pcol[:, :], [[0, 1]], 0, 1)
        iota(iota_p[:, :], [[1, 128]])
        t_iota = iota(tile_no[:, :, :], [[NT, 2], [1, NT]], 1)
        t_ones, t_hp = t[4], t[6]

        t_silu = act(lambda e: e.activation(CS, CS, ACT.Silu), t_c)
        pT = bank(0, 2, 2, 8)
        for l in range(2):
            for k in range(2):
                t_tp = tp(pT[:, l, k, :], CS[:, l, k * 128:(k + 1) * 128], t_silu, t_id, mark=True, n=8)
        t_cT = copy(dve, cT, pT, t_tp)
        modt, t_mods, t_row = [], [], [None] * 3

        def mod_columns(l):
            pc = bank(4, 4, 8)
            for blk in range(4):
                for k in range(2):
                    t_m = mm(pc[:, blk, :], WM[:, l, k, 128 * blk:128 * blk + 128], cT[:, l, k, :],
                             k == 0, k == 1, t_cT, t_wm[l], modt, mark=(k == 1))
            yield
            a = copy(dve, modT[:, l, :, :], pc, t_m)
            modt.append(dve(lambda e: e.tensor_scalar(modT[:, l, 2:4, :], modT[:, l, 2:4, :], 1.0, None, ALU.add), a))

        def mod_rows(l, j):
            for k in range(2):
                t_m = mm(ps[1 + j][0:8, :], cT[:, l, k, :], WM[:, l, k, 512 * j:512 * j + 512],
                         k == 0, k == 1, t_cT, t_wm[l], t_row[j], mark=(k == 1))
            yield
            t_row[j] = copy(dve, MOD[:, l, 512 * j:512 * j + 512], ps[1 + j][0:8, :], t_m)

        gview = MOD.rearrange("b l (u v d) -> b l u v d", u=2, v=3)[:, :, :, 2, :]
        cview = MOD.rearrange("b l (u v d) -> b l u v d", u=2, v=3)[:, :, :, 1, :]

        def mod_gates(l):
            g = gview[:, l]
            t1 = dve(lambda e: e.tensor_scalar(GT[:, l], g, -1.0, None, ALU.mult), t_row)
            t1 = tt(dve, GT[:, l], GT[:, l], g, ALU.max, t1)
            t1 = dve(lambda e: e.tensor_scalar(GT[:, l], GT[:, l], 0.25, None, ALU.max), t1)
            t2 = dve(lambda e: e.tensor_scalar(g, g, 0.0, 2.0, ALU.is_ge, ALU.mult), t1)
            t2 = dve(lambda e: e.scalar_tensor_tensor(out=g, in0=g, scalar=-1.0, in1=GT[:, l],
                                                      op0=ALU.add, op1=ALU.mult), t2)
            t_mods.append(dve(lambda e: e.tensor_scalar(cview[:, l], cview[:, l], 1.0, None, ALU.add), t2))

        bn_last = [None] * 4

        def tile_stats(i, *ready):
            r = i % 4
            a = dve(lambda e: e.bn_stats(bnst[:, r, :], X[:, i, :]), bn_last[r], *ready)
            bn_last[r] = dve(lambda e: e.bn_aggr(stat[:, i, :], bnst[:, r, :]), a)
            return bn_last[r]

        def rstd_of(i, j, *ready):
            a = dve(lambda e: e.tensor_scalar(rstd[:, i:j], stat[:, i:j, 1], 1e-5, None, ALU.add), *ready)
            a = act(lambda e: e.activation(rstd[:, i:j], rstd[:, i:j], ACT.Sqrt), a)
            return dve(lambda e: e.reciprocal(rstd[:, i:j], rstd[:, i:j]), a)

        def xnorm(dst, i, *after):
            return dve(lambda e: e.tensor_scalar(dst, X[:, i, :], stat[:, i, 0:1], rstd[:, i:i + 1],
                                                 ALU.subtract, ALU.mult), *after)

        def settled(i, y, t_rstd, n=8):
            a = tile_stats(i, y)
            if i % n == n - 1:
                t_rstd.extend([rstd_of(i + 1 - n, i + 1, a)] * n)

        lo_by = [pool, pool]

        def norm_T(l, place, rings, banks, t_stats, tiles, ends):
            xn_ring, v_ring = rings
            got = {}

            def first(n):
                xn, free, users = xn_ring.next()
                got[n] = xn, xnorm(xn, tiles[n], t_stats(tiles[n]), free), users

            def second(n):
                xn, a, users = got[n]
                bk, bfree, busers = banks.next()
                for k in range(2):
                    m = tp(bk[:, k * 128:(k + 1) * 128], xn[:, k * 128:(k + 1) * 128], a, bfree, mark=(k == 1))
                users.append(m)
                got[n] = bk, m, busers

            def third(n):
                bk, m, busers = got[n]
                b = tiles[n] // 4
                v, vfree, vusers = v_ring.next()
                a = []
                for k in range(2):
                    src, add, by = bk[:, k * 128:(k + 1) * 128], modT[:, l, k, b:b + 1], modT[:, l, 2 + k, b:b + 1]
                    if l == 0 and n % 2:
                        a.append(dve(lambda e, k=k, src=src, add=add, by=by: e.tensor_scalar(
                            v[:, k, :], src, by, add, ALU.mult, ALU.add), m, modt[l], vfree))
                    else:
                        a.append(act(lambda e, k=k, src=src, add=add, by=by: e.activation(
                            v[:, k, :], src, ACT.Identity, bias=add, scale=by), m, modt[l], vfree))
                busers.extend(a)
                got[n] = v, a, vusers

            def fourth(n):
                v, a, vusers = got[n]
                hi, lo, src = place(n, v)
                got[n] = hi, lo, src, copy(act, hi, src, a), vusers

            def fifth(n):
                hi, lo, src, a, vusers = got.pop(n)
                a = tt(lo_by[l], lo, src, hi, ALU.subtract, a)
                vusers.append(a)
                ends.append(a)

            return [first, second, third, fourth, fifth]

        def gates(l, which, bk, b, *after):
            return mm(bk[:, 0:256], sel[0:8, b, :], MOD[0:8, l, (2 + 3 * which) * D:(3 + 3 * which) * D],
                      True, True, t_mods[l], t_sel, *after, mark=True)

        def slab_list(l):
            E, ins = ((4, ((w1_in, 2), (w3_in, 2), (w2_in, 8))), (8, ((v1_in, 2), (v2_in, 8))))[l]
            return [(x, n, w[x].rearrange("(k p) n -> p k n", p=128), k) for x in range(E) for n, (w, k) in enumerate(ins)]

        WD = [dram("WD0", [128, 4 * 3 * 4096], f16), dram("WD1", [128, 8 * 2 * 4096], f16)]
        st_sem = [sem(f"l_st{i}") for i in range(2)]
        sv_sem = [sem(f"l_sv{i}") for i in range(2)]
        conv_n = [0]

        def converter(l, stage, halves, q_lo):
            nslab = (3, 2)[l]
            todo = [(*slab, hf) for slab in slab_list(l) for hf in range(2)]
            got = {}

            def load(c):
                x, n, src, k, hf = todo[c]
                st, free, users = stage.next()
                got[c] = st, sp.dma(st_sem[c % 2], shaped(st, (k // 2, 2048 // k)),
                                    src[:, hf * k // 2:(hf + 1) * k // 2, :], free), users

            def step(c):
                if c == 0:
                    load(0)
                if c + 1 < len(todo):
                    load(c + 1)
                x, n, src, k, hf = todo[c]
                st, a, users = got.pop(c)
                pr, pfree, pusers = halves.next()
                s_ = split(pr, st, q_lo, a, pfree)
                users.extend(s_)
                for m in range(2):
                    at = (x * 2 * nslab + m * nslab + n) * 2048 + hf * 1024
                    pusers.append(sp.dma(sv_sem[c % 2], WD[l][:, at:at + 1024], pr[m], s_))

            return [lambda c=c: step(c) for c in range(len(todo))]

        area = Area(0)
        hTh, hTl = area.pair(2, T)
        QC = area(NT, 32)
        QS = area(NT, 32)
        TH = area(NT, 32)
        DN = TH[:, 0:16, :].rearrange("p a b -> p (a b)").rearrange("p (t n) -> p t n", n=16)
        D2 = TH[:, 16:32, :].rearrange("p a b -> p (a b)").rearrange("p (t n) -> p t n", n=16)
        Wqk, Wv, Wo = area.pair(2, 32), area.pair(2, 1024), area.pair(8, D)
        stage = area.ring(2, 1024)
        halves = area.pairs(2, 1024)
        YG = area.ring(2, D)
        GB = area(8, D)
        lap = area.at
        assert lap <= 22912, lap
        ts = []

        def x_stats(i):
            a = tile_stats(i, xt[i // 8])
            if i % 4 == 3:
                ts.extend([rstd_of(i - 3, i + 1, a)] * 4)

        for i in range(8):
            x_stats(i)
        for _ in mod_columns(0):
            pass
        t_w = []

        def weight(pair, a, b):
            t_w.extend(split([w.rearrange("p a b -> p (a b)") for w in pair], wst[:, a:b], dve, t_lw))

        tr = Ring([ps[6], ps[7]])
        area = Area(mod_end + 4160)
        xn0, vr0 = area.ring(6, D), area.ring(5, 2, 128)
        t_hT = []
        stages = norm_T(0, lambda n, v: (hTh[:, :, n * 128:(n + 1) * 128], hTl[:, :, n * 128:(n + 1) * 128], v),
                        (xn0, vr0), tr, lambda i: ts[i], range(NT), t_hT)
        qkp = [bank(i, 16, 32) for i in (0, 5)]
        t_qks = []

        def hT_of(i, k):
            return hTh[:, k, i * 128:(i + 1) * 128], hTl[:, k, i * 128:(i + 1) * 128]

        def qk_of(i):
            for k in range(2):
                m = mm3(qkp[i // 16][:, i % 16, :], hT_of(i, k), (Wqk[0][:, k, :], Wqk[1][:, k, :]),
                        k == 0, k == 1, t_hT[i], t_w, t_cT, mark=(k == 1))
            t_qks.append(m)

        grb = Ring([ps[1], ps[2], ps[3]])

        def gate_rows(b):
            bk, bfree, busers = grb.next()
            g = gates(0, 0, bk, b, t_row, bfree)
            yield
            a = copy(dve, GB[:, b, :], bk[:, 0:256], g)
            busers.append(a)

        def later(f, *args):
            yield
            f(*args)

        mods = {4: later(weight, Wqk, 0, 64), 7: later(weight, Wv, 64, 2112), 9: later(weight, Wo, 2112, 4160),
                3: mod_rows(0, 0), 6: mod_rows(0, 1), 8: mod_rows(0, 2), 11: mod_columns(1), 13: mod_rows(1, 0),
                15: mod_rows(1, 1), 17: mod_rows(1, 2), 19: later(mod_gates, 0), 22: later(mod_gates, 1)}
        for b in range(8):
            mods[24 + b] = gate_rows(b)
        idle = lambda n: None
        stages = [stages[0], idle, *stages[1:4], idle, stages[4], idle, qk_of]
        for t in range(NT + len(stages) - 1):
            if t + 8 < NT:
                x_stats(t + 8)
            for n in (t - 1, t):
                if n in mods:
                    next(mods[n], None)
            pipeline(NT, stages, t, t + 1)
        t_qk = t_qks[-1]
        t_mod_done = now(pe, dve, act)
        t_th = [act(lambda e, j=j: e.activation(TH[:, 16 * j:16 * j + 16, :], qkp[j], ACT.Tanh), t_qk) for j in range(2)]
        t_qc = act(lambda e: e.activation(QC, TH, ACT.Sin, bias=half_pi[:, 0:1], scale=PI / 4), t_th, t_hp)
        t_qs = act(lambda e: e.activation(QS, TH, ACT.Sin, scale=PI / 4), t_th)
        area = Area(lap)
        KVF = area.ring(2, 2, 1024)
        KVP = area.pairs(3, 2, 1024)
        cks = view(area.at, 2, 2, NT, 16, dt=f16)
        TM = area.ring(2, 2, 1024)
        HT = area.pairs(2, 8, 128)
        cumb = [bank(2 + j, 8, 4, 16) for j in range(2)]
        tks = [split((cks[:, 0, j], cks[:, 1, j]), src[:, :, 16:32], dve, tq, t_mod_done, t_w)
               for j, src, tq in ((0, QC, t_qc), (1, QS, t_qs))]
        vr = Ring([ps[4], ps[5]])
        vr.free = [list(modt), list(t_th)]
        tr2 = tr
        t_kv0 = now(pe, dve, act, pool)

        def heads_of(ap, n=8):
            return ap.rearrange("p (h e) -> p h e", e=64)

        def l0_values(i):
            kvf, free, users = KVF.next()
            kvp, pfree, pusers = KVP.next()
            ends = []
            for hf in range(2):
                bk, bfree, busers = vr.next()
                for k in range(2):
                    a = mm3(bk[:, :], hT_of(i, k), [w[:, k, hf * 512:hf * 512 + 512] for w in Wv],
                            k == 0, k == 1, bfree, mark=(k == 1))
                for j, q in ((0, QC), (1, QS)):
                    cut = slice(hf * 512, hf * 512 + 512)
                    f = tt(dve, heads_of(kvf[:, j, cut]), heads_of(bk[:, :]),
                           bc(q[:, i, 16 + 8 * hf:24 + 8 * hf], 2, 64), ALU.mult, a, free, t_kv0)
                    busers.append(f)
                    s_ = split((kvp[0][:, j, cut], kvp[1][:, j, cut]), kvf[:, j, cut], pool, f, pfree)
                    users.extend(s_)
                    ends.extend(s_)
            return kvp, ends, pusers

        vals = [l0_values(0)]
        for j in range(2):
            for m in range(2):
                s4 = cks[:, m, j].rearrange("p (b c) n -> p b c n", c=4)
                mm(cumb[j], tri[:, :], s4, m == 0, False, tks[j], t_tri, t_ones)
                for back in range(1, 4):
                    for b in range(8):
                        end = m == 1 and back == 3 and b == 7
                        t_cum = mm(cumb[j][:, b, back:4, :], ones[:, :], s4[:, b, 0:4 - back, :], False, end, mark=end)
        cumc = bank(2, NT, 16)
        cums = bank(3, NT, 16)
        a = tt(dve, DN, QC[:, :, 0:16], cumc, ALU.mult, t_cum)
        b_ = tt(dve, D2, QS[:, :, 0:16], cums, ALU.mult, t_cum)
        a = dve(lambda e: e.scalar_tensor_tensor(out=DN, in0=DN, scalar=1e-6, in1=D2, op0=ALU.add, op1=ALU.add), a, b_)
        a = dve(lambda e: e.reciprocal(DN, DN), a)
        b_ = tt(dve, QC[:, :, 0:16], QC[:, :, 0:16], DN, ALU.mult, a)
        t_q = tt(dve, QS[:, :, 0:16], QS[:, :, 0:16], DN, ALU.mult, a)
        acc_free = [t_q, b_]
        vals.append(l0_values(1))

        def l0_out(i, hd, t_hd, hd_users):
            ht, hfree, husers = HT.next()
            cp = []
            for q in range(2):
                bk, bfree, busers = tr2.next()
                for j in range(4):
                    a = tp(bk[:, j * 128:(j + 1) * 128], hd[:, (4 * q + j) * 128:(4 * q + j + 1) * 128], t_hd, bfree,
                           mark=(j == 3))
                hd_users.append(a)
                s_ = split([h[:, 4 * q:4 * q + 4, :] for h in ht], bk[:, :].rearrange("p (j n) -> p j n", j=4), dve, a, hfree)
                busers.extend(s_)
                cp.append(s_)
            return ht, cp, husers

        def l0_proj(i, ht, cp, husers):
            bk, bfree, busers = vr.next()
            for j in range(8):
                m = mm3(bk[:, 0:256], [h[:, j, :] for h in ht], [w[:, j, :] for w in Wo],
                        j == 0, j == 7, cp[j // 4], bfree, mark=(j == 7))
            husers.append(m)
            yg, yfree, yusers = YG.next()
            y = tt(dve, yg, bk[:, 0:256], GB[:, i // 4, :], ALU.mult, m, yfree)
            busers.append(y)
            y = tt(dve, X[:, i, :], X[:, i, :], yg, ALU.add, y)
            yusers.append(y)
            return y

        t_x = []
        late = None
        steps = converter(0, stage, halves, pool)
        for i in range(NT):
            kv, ends, kusers = vals[i]
            first = i % 4 == 0
            for j in range(2):
                for hf in range(2):
                    for m2 in range(2):
                        end = j == 1 and hf == 1 and m2 == 1
                        m = mm(ps[2 * j + hf][:, :], tri[:, :], kv[m2][:, j, hf * 512:hf * 512 + 512],
                               first and m2 == 0, False, ends, acc_free, mark=end)
            tm, tfree, tusers = TM.next()
            reads = []
            for j, q in ((0, QC), (1, QS)):
                for hf in range(2):
                    reads.append(tt(dve, heads_of(tm[:, j, hf * 512:hf * 512 + 512]), heads_of(ps[2 * j + hf][:, :]),
                                    bc(q[:, i, 8 * hf:8 * hf + 8], 2, 64), ALU.mult, m, tfree))
            if late is not None:
                got = l0_out(*late)
            if i + 2 < NT:
                vals.append(l0_values(i + 2))
            acc_free = reads
            if i % 4 != 3:
                for j in range(2):
                    for hf in range(2):
                        for m2 in range(2):
                            end = j == 1 and hf == 1 and m2 == 1
                            m = mm(ps[2 * j + hf][:, :], atri[:, :], kv[m2][:, j, hf * 512:hf * 512 + 512], False, True,
                                   reads, t_atri, mark=end)
            kusers.append(m)
            t_hd = tt(dve, tm[:, 0], tm[:, 0], tm[:, 1], ALU.add, reads)
            if late is not None:
                settled(late[0], l0_proj(late[0], *got), t_x)
            late = (i, tm[:, 0], t_hd, tusers)
            if 2 <= i < 2 + len(steps):
                steps[i - 2]()
        got = l0_out(*late)
        settled(late[0], l0_proj(late[0], *got), t_x)
        t_conv = [[(s_, s_.n) for s_ in sv_sem]]

        def moe(l, E, CH, w_rt, b_rt, gated, ready, t_x, t_wd, outs, beside, feed=None):
            NS = CH * NT + E - 1
            nslab = 3 if gated else 2
            span = 2 * nslab * 2048
            HB = dram(f"HB{l}", [T, 2 * D], f16)
            YT = dram(f"YT{l}", [(CH * NT + NS) * 128, D])
            area = Area(E * span // 2)
            SL = [area(NT) for c in range(CH)]
            GV = [area(NT) for c in range(CH)]
            ei = area(NS).bitcast(i32)
            gi = area(NS).bitcast(i32)
            yi = area(NS).bitcast(i32)
            base = area.at
            l_r = sem(f"l_r{l}")
            RWf = area(2, E)
            RW = area.pair(2, E)
            RB = area(E)
            sp.dma(l_r, RWf, w_rt.rearrange("(k p) n -> p k n", p=128), ready)
            t_r = sp.dma(l_r, RB, b_rt.unsqueeze(0).broadcast_to([128, E]), ready)
            t_rw = []
            LG = area(NT, E)
            HR = area.ring(4, D)
            HP = area.ring(4, 2, D, dt=f16)
            HTR = area.ring(2, 4, 128, dt=f16)
            assert not l or area.at <= 35968
            HBv = HB.rearrange("(t p) d -> p t d", p=128)
            everything = [*ready, *now()]
            trb = Ring([ps[6], ps[7]])
            trb.free = [list(everything) for _ in range(2)]
            scb = Ring([ps[4], ps[5]])
            scb.free = [list(everything) for _ in range(2)]
            lgp = bank(0, NT, E)
            l_hb = [sem(f"l_hb{l}_{i}") for i in range(4)]
            l_ew = sem(f"l_ew{l}")
            t_ew = []

            def weights_in(i):
                if l and i >= 20:
                    i = i + 1 if i < 31 else 20
                n = E * span // 32
                t_ew.append(sp.dma(l_ew, BIG16[:, i * n:(i + 1) * n], WD[l][:, i * n:(i + 1) * n], ready, t_wd,
                                   t_feed if i == 20 else None))

            def rows_T(src, *after):
                bk, bfree, busers = trb.next()
                b16 = shaped(bk[:, 0:256].bitcast(f16), (4, 128))
                for k in range(4):
                    m = tp16(b16[:, k, :], src[:, k * 128:(k + 1) * 128], *after, bfree, mark=(k == 3))
                return b16, m, busers

            got, t_lg, t_feed = {}, [], None

            def scale_rows(b):
                sc, sfree, susers = scb.next()
                got[f"sc{b}"] = sc, susers, mm(sc[:, :], sel[0:8, b, :], MOD[0:8, l, 3 * D:5 * D], True, True,
                                               t_mods[l], t_sel, sfree, mark=True)

            def h_rows(i):
                b = i // 4
                if i == 2:
                    t_rw.extend(split([w.rearrange("p a b -> p (a b)") for w in RW],
                                      RWf.rearrange("p a b -> p (a b)"), dve, t_r, ready))
                if i % 4 == 2 and b < 7:
                    scale_rows(b + 1)
                sc, susers, t_sc = got[f"sc{b}"]
                h, hfree, husers = HR.next()
                a = dve(lambda e: e.scalar_tensor_tensor(out=h, in0=X[:, i, :], scalar=stat[:, i, 0:1], in1=sc[:, 256:512],
                                                         op0=ALU.subtract, op1=ALU.mult), t_x[i], t_sc, hfree, ready)
                a = dve(lambda e: e.scalar_tensor_tensor(out=h, in0=h, scalar=rstd[:, i:i + 1], in1=sc[:, 0:256],
                                                         op0=ALU.mult, op1=ALU.add), a)
                if i % 4 == 3:
                    susers.append(a)
                got[i] = h, a, husers

            def h_split(i):
                h, a, husers = got[i]
                hp, pfree, pusers = HP.next()
                s_ = split((hp[:, 0, :], hp[:, 1, :]), h, pool, a, pfree)
                husers.extend(s_)
                flat = hp.rearrange("p a b -> p (a b)")
                pusers.append(sp.dma(l_hb[i % 4], HBv[:, i, :], flat, s_))
                if l == 0 and i >= 22:
                    weights_in(i - 22)
                if l and i < 25:
                    weights_in(i + 6)
                got[i] = flat, s_, pusers

            def h_turn(i):
                flat, s_, pusers = got[i]
                b16, m, busers = rows_T(flat, s_)
                pusers.append(m)
                got[i] = b16, m, busers

            def h_copy(i):
                b16, m, busers = got[i]
                ht, tfree, tusers = HTR.next()
                a = copy(act, ht, b16, m, tfree)
                busers.append(a)
                got[i] = ht, a, tusers

            def logits(i):
                ht, a, tusers = got.pop(i)
                for k in range(2):
                    m = mm3(lgp[:, i, :], (ht[:, k, :], ht[:, 2 + k, :]), [w[:, k, :] for w in RW], k == 0, k == 1,
                            a, t_rw, everything, mark=(k == 1))
                tusers.append(m)
                t_lg.append(m)

            scale_rows(0)
            stages = [h_rows, lambda i: None, h_split, lambda i: None, h_turn, h_copy, logits]
            if feed:
                for t in range(12):
                    if t < 6:
                        next(feed)
                        weights_in(t)
                for t in range(NT + len(stages) - 1):
                    next(feed, None)
                    pipeline(NT, stages, t, t + 1)
                t_feed = now()
            else:
                pipeline(NT, stages)
                t_feed = None
            for i in range(len(t_ew), 32):
                weights_in(i)
            m = t_lg[-1]
            t_hb = [(s_, s_.n) for s_ in l_hb]
            cur = tt(dve, LG, lgp, bc(RB, 1, NT), ALU.add, m, t_r)
            late_words = area.at
            MX, W3, PR = area(NT), area(NT, E), area(NT, E)
            AL = area(NT, E, dt=f16)
            OH = [area(NT, E) for _ in range(CH)]
            dec = area(E)
            t_io = iota(dec, [[-1, E]], E, 0, ready)
            if CH == 2:
                cur = dve(lambda e: e.tensor_reduce(MX, LG, AX.X, ALU.max), cur)
                cur = tt(dve, PR, LG, bc(MX, 2, E), ALU.subtract, cur)
                cur = act(lambda e: e.activation(PR, PR, ACT.Exp), cur)
                cur = dve(lambda e: e.tensor_reduce(MX, PR, AX.X, ALU.add), cur)
                cur = dve(lambda e: e.reciprocal(MX, MX), cur)
                cur = tt(dve, PR, PR, bc(MX, 2, E), ALU.mult, cur)
            else:
                cur = act(lambda e: e.activation(PR, LG, ACT.Sigmoid), cur)
            for c in range(CH):
                cur = dve(lambda e, c=c: e.tensor_reduce(GV[c], PR, AX.X, ALU.max), cur)
                cur = tt(dve, W3, PR, bc(GV[c], 2, E), ALU.is_ge, cur)
                cur = tt(dve, W3, W3, bc(dec, 1, NT), ALU.mult, cur, t_io)
                cur = dve(lambda e: e.tensor_reduce(MX, W3, AX.X, ALU.max), cur)
                cur = tt(dve, OH[c], W3, bc(MX, 2, E), ALU.is_equal, cur)
                if c + 1 < CH:
                    cur = dve(lambda e, c=c: e.scalar_tensor_tensor(out=PR, in0=OH[c], scalar=-2.0, in1=PR,
                                                                    op0=ALU.mult, op1=ALU.add), cur)
            if CH == 2:
                cur = tt(dve, MX, GV[0], GV[1], ALU.add, cur)
                cur = dve(lambda e: e.reciprocal(MX, MX), cur)
                for c in range(2):
                    cur = tt(dve, GV[c], GV[c], MX, ALU.mult, cur)
                cur = tt(dve, AL, OH[0], OH[1], ALU.add, cur)
            else:
                cur = copy(dve, AL, OH[0], cur)
            rk, ct = bank(1, NT, E), bank(2, NT, E)
            mm(rk, stri[:, :], AL, True, True, cur, t_stri, t_ones)
            m = mm(ct, ones[:, :], AL, True, True, mark=True)
            CI, zz, cs = area(E, NT), area(NT), area(E, NT)
            cur = dve(lambda e: e.memset(zz, 0.0), m)
            cur = copy(dve, cs, ct.rearrange("p t e -> p e t"), cur)
            for x in range(E):
                t_last = dve(lambda e, x=x: e.tensor_tensor_scan(out=CI[:, x, :], data0=cs[:, x, :], data1=zz, initial=0.0,
                                                                 op0=ALU.add, op1=ALU.add), cur)
            n_i = area(E).bitcast(i32)
            n_p, ends_, bases = area(E), area(E), area(E)
            cur = dve(lambda e: e.tensor_scalar(n_p, CI[:, :, NT - 1], 127.0, None, ALU.add), t_last)
            cur = copy(dve, n_i, n_p, cur)
            cur = dve(lambda e: e.tensor_scalar(n_i, n_i, 7, 7, ALU.arith_shift_right, ALU.arith_shift_left), cur)
            cur = copy(dve, n_p, n_i, cur)
            cur = dve(lambda e: e.tensor_tensor_scan(out=ends_, data0=n_p, data1=zz[:, 0:E], initial=0.0,
                                                     op0=ALU.add, op1=ALU.add), cur)
            cur = tt(dve, bases, ends_, n_p, ALU.subtract, cur)
            cur = tt(dve, CI, CI, cs, ALU.subtract, cur)
            cur = tt(dve, CI, CI, bc(bases, 2, NT), ALU.add, cur)
            PS_ = area(NT, E)
            cur = tt(dve, PS_, rk, CI.rearrange("p e t -> p t e"), ALU.add, cur)
            for c in range(CH):
                cur = tt(dve, W3, PS_, OH[c], ALU.mult, cur)
                cur = dve(lambda e, c=c: e.tensor_reduce(SL[c], W3, AX.X, ALU.add), cur)
            it = area(NS)
            ex = area(NS)
            it128 = area(NS)
            t_it = iota(it, [[1, NS]], 0, 0, ready)
            t_it = iota(it128, [[128, NS]], 0, 0, ready)
            lap = Area(base) if l else area
            if l:
                dve.wait(now(pe, act, pool), t_hb)
            cmp_ = lap(NS, E)
            cur = tt(dve, cmp_, bc(ends_, 1, NS), bc(it128, 2, E), ALU.is_le, cur, t_it)
            cur = dve(lambda e: e.tensor_reduce(ex, cmp_, AX.X, ALU.add), cur)
            cur = dve(lambda e: e.tensor_scalar(ex, ex, float(E - 1), float(span), ALU.min, ALU.mult), cur)
            t_ei = copy(dve, ei, ex, cur)
            s_i, s_lo, s_hi = area(NT).bitcast(i32), area(NT), area(NT)
            s_j = area(NT).bitcast(i32)
            G = 8
            S1 = lap.ring(3, G, 128, dt=f16)
            A1 = lap.ring(3, G, 2, NS, dt=f16)
            assert not l or lap.at <= late_words
            mp = bank(3, 2, NS)
            cur = t_ei
            for c in range(CH):
                cur = copy(dve, s_i, SL[c], cur)
                cur = dve(lambda e: e.tensor_scalar(s_j, s_i, 7, None, ALU.arith_shift_right), cur)
                cur = copy(dve, s_hi, s_j, cur)
                cur = dve(lambda e, c=c: e.scalar_tensor_tensor(out=s_lo, in0=s_hi, scalar=-128.0, in1=SL[c],
                                                                op0=ALU.mult, op1=ALU.add), cur)
                for g in range(0, NT, G):
                    s1, sfree, susers = S1.next()
                    a1, afree, ausers = A1.next()
                    v = tt(dve, a1[:, :, 0, :], bc(s_hi[:, g:g + G], 2, NS), bc(it, 1, G), ALU.is_equal, cur, afree)
                    w = dve(lambda e, a1=a1: e.tensor_scalar(a1[:, :, 1, :], a1[:, :, 0, :], pcol[:, 0:1], None, ALU.mult), v)
                    v = tt(pool, a1[:, :, 0, :], a1[:, :, 0, :], bc(tile_no[:, c, g:g + G], 2, NS), ALU.mult, w)
                    u = tt(dve, s1, bc(s_lo[:, g:g + G], 2, 128), bc(iota_p[:, :], 1, G), ALU.is_equal, cur, sfree, t_iota)
                    for n in range(G):
                        m = mm(mp, s1[:, n, :], a1[:, n, :, :], c == 0 and g == 0 and n == 0, c == CH - 1 and g == NT - G and n == G - 1,
                               u, v, everything, mark=(n == G - 1))
                    susers.append(m)
                    ausers.append(m)
                    cur = u
            rf, pad = area(NS), area(NS)
            slot_no = area(NS)
            t_sn = iota(slot_no, [[128, NS]], CH * NT * 128, 1, ready)
            r_i = area(NS).bitcast(i32)
            cur = dve(lambda e: e.tensor_scalar(pad, mp[:, 0, :], 1.0, None, ALU.is_lt), m)
            cur = dve(lambda e: e.tensor_scalar(rf, mp[:, 0, :], 128.0, -128.0, ALU.mult, ALU.add), cur)
            cur = tt(dve, rf, rf, mp[:, 1, :], ALU.add, cur)
            cur = copy(dve, r_i, rf, cur)
            t_gi = dve(lambda e: e.tensor_scalar(gi, r_i, T - 1, None, ALU.bitwise_and), cur)
            cur = tt(dve, slot_no, slot_no, rf, ALU.subtract, cur, t_sn)
            cur = tt(dve, slot_no, slot_no, pad, ALU.mult, cur)
            cur = tt(dve, rf, rf, slot_no, ALU.add, cur)
            t_yi = copy(dve, yi, rf, cur)

            area = Area(base)
            HIN = area.ring(3, 2 * D, dt=f16)
            HTT = area.ring(2, 4, 128, dt=f16)
            UP = area.ring(2, 1024)
            UPT = area.pairs(1 if l else 2, 8, 128)
            YO = area.ring(2, D)
            if l == 0:
                st_, hv_ = area.ring(2, 1024), area.pairs(2, 1024)
            everything = now()
            for q in (act, dve, pe, pool, sp):
                q.wait(everything, t_hb)
            wide = Ring([ps[0], ps[1], ps[2], ps[3]])
            trb = Ring([ps[6], ps[7]])
            yb = Ring([ps[4], ps[5]])
            l_hi = [sem(f"l_hi{l}_{i}") for i in range(3)]
            l_yo = [sem(f"l_yo{l}_{i}") for i in range(2)]
            regs = {}

            def reg(j):
                def f(e):
                    regs.pop(j - 3, None)
                    regs[j] = e.value_load(ei[0:1, j:j + 1], min_val=0, max_val=(E - 1) * span)
                pe.wait(t_ei, t_ew[-1])
                pe.items.append(f)

            def mm_w(out, lhs, j, at, n, start, stop, *after, mark=False):
                for p, (m, w) in enumerate(((0, 0), (0, 1), (1, 0))):
                    r = pe(lambda e, m=m, w=w, p=p: e.matmul(
                        out, lhs[m], BIG16[:, bass.ds(regs[j] + (w * nslab * 2048 + at), n)],
                        start=start and p == 0, stop=stop and p == 2, skip_group_check=True),
                        *after, mark=mark and p == 2)
                return r

            def fetch(j):
                h, hfree, husers = HIN.next()
                return h, pool.gather(l_hi[j % 3], h, HB, gi[:, j:j + 1], t_gi, t_hb, hfree), husers

            def turn(j, h, a, husers):
                b16, m, busers = rows_T2(h, a)
                husers.append(m)
                ht, tfree, tusers = HTT.next()
                a = copy(act, ht, b16, m, tfree)
                busers.append(a)
                return ht, a, tusers

            def rows_T2(src, *after):
                bk, bfree, busers = trb.next()
                b16 = shaped(bk[:, 0:256].bitcast(f16), (4, 128))
                for k in range(4):
                    m = tp16(b16[:, k, :], src[:, k * 128:(k + 1) * 128], *after, bfree, mark=(k == 3))
                return b16, m, busers

            def up(j, hf, ht, a, u, ufree):
                bks = []
                for w in range(2 if gated else 1):
                    bk, bfree, busers = wide.next()
                    for k in range(2):
                        m = mm_w(bk[:, :], (ht[:, k, :], ht[:, 2 + k, :]), j, 2048 * w + 1024 * k + 512 * hf, 512,
                                 k == 0, k == 1, a, bfree, mark=(k == 1))
                    bks.append((bk, m, busers))
                us = u[:, hf * 512:hf * 512 + 512]
                bk, m, busers = bks[0]
                s_ = act(lambda e: e.activation(us, bk[:, :], ACT.Silu if gated else ACT.Gelu), m, ufree)
                busers.append(s_)
                if gated:
                    bk2, m2, busers2 = bks[1]
                    s_ = tt(dve, us, us, bk2[:, :], ALU.mult, s_, m2)
                    busers2.append(s_)
                return s_, bks[-1][1]

            def u_T(u, parts, uusers):
                ut, tfree, tusers = UPT.next()
                cp = []
                for q in range(2):
                    bk, bfree, busers = trb.next()
                    for n in range(4):
                        m = tp(bk[:, n * 128:(n + 1) * 128], u[:, (4 * q + n) * 128:(4 * q + n + 1) * 128],
                               parts[q], bfree, mark=(n == 3))
                    uusers.append(m)
                    s_ = split([h[:, 4 * q:4 * q + 4, :] for h in ut], bk[:, :].rearrange("p (j n) -> p j n", j=4),
                               dve, m, tfree)
                    busers.extend(s_)
                    cp.append(s_)
                return ut, cp, tusers

            def down(j, ut, cp, tusers):
                bk, bfree, busers = yb.next()
                for n in range(8):
                    m = mm_w(bk[:, 0:256], [h[:, n, :] for h in ut], j, (nslab - 1) * 2048 + 256 * n, 256, n == 0, n == 7,
                             cp[n // 4], bfree, mark=(n == 7))
                tusers.append(m)
                y, yfree, yusers = YO.next()
                a = copy(act, y, bk[:, 0:256], m, yfree)
                busers.append(a)
                yusers.append(pool.scatter(l_yo[j % 2], YT, yi[:, j:j + 1], y, a, t_yi))

            fetched = [fetch(0), fetch(1)]
            turned = turn(0, *fetched[0])
            reg(0)
            late = None
            if l == 0:
                steps = converter(1, st_, hv_, pool)
            for j in range(NS):
                ht, t_ht, tusers = turned
                if j + 1 < NS:
                    reg(j + 1)
                u, ufree, uusers = UP.next()
                p0, _ = up(j, 0, ht, t_ht, u, ufree)
                if late:
                    got = u_T(*late)
                p1, m = up(j, 1, ht, t_ht, u, ufree)
                tusers.append(m)
                if j + 2 < NS:
                    fetched.append(fetch(j + 2))
                if j + 1 < NS:
                    turned = turn(j + 1, *fetched[j + 1])
                if late:
                    down(j - 1, *got)
                late = (u, (p0, p1), uusers)
                if l == 0 and j % 2 == 0 and j // 2 < len(steps):
                    steps[j // 2]()
            got = u_T(*late)
            down(NS - 1, *got)
            t_ys = [(s_, s_.n) for s_ in l_yo]
            area = Area(base)
            YI = area.ring(3, CH, 4, D)
            l_yi = [sem(f"l_yi{l}_{i}") for i in range(3)]
            gb = Ring([ps[3], ps[4], ps[5]])
            everything = now()
            if beside:
                phase_sems(2)
                next(beside)
            YTv = YT[0:CH * T, :].rearrange("(c t p) d -> p c t d", c=CH, p=128)
            got = {}

            def rows_in(g):
                gk, gfree, gusers = gb.next()
                t_g = gates(l, 1, gk, g, gfree, everything)
                y4, yfree, yusers = YI.next()
                for c in range(CH):
                    t_y4 = sp.dma(l_yi[g % 3], y4[:, c], YTv[:, c, 4 * g:4 * g + 4, :], t_ys, yfree, everything)
                got[g] = gk, t_g, gusers, y4, t_y4, yusers

            def combine(i):
                gk, t_g, gusers, y4, t_y4, yusers = got[i // 4]
                y = y4[:, 0, i % 4, :]
                a = act(lambda e: e.activation(y, y, ACT.Copy, scale=GV[0][:, i:i + 1]), t_y4)
                if CH == 2:
                    y2 = y4[:, 1, i % 4, :]
                    a = dve(lambda e: e.scalar_tensor_tensor(
                        out=y, in0=y2, scalar=GV[1][:, i:i + 1], in1=y, op0=ALU.mult, op1=ALU.add), a)
                a = tt(dve, y, y, gk[:, 0:256], ALU.mult, a, t_g)
                if i % 4 == 3:
                    gusers.append(a)
                a = tt(pool if l == 0 or i % 2 else dve, X[:, i, :], X[:, i, :], y, ALU.add, a)
                got[i + 100] = a
                if i % 4 == 3:
                    yusers.append(a)
                if l:
                    finished(i, a)

            def stats_in(i):
                if l == 0:
                    settled(i, got.pop(i + 100), outs)

            for g in range(3):
                rows_in(g)
            for i in range(NT + 1):
                if i < NT:
                    combine(i)
                if i % 4 == 3 and i // 4 + 3 < NT // 4:
                    rows_in(i // 4 + 3)
                if i:
                    stats_in(i - 1)
                if i >= 16 and beside:
                    next(beside)

        l_o = sem("l_o")
        ov = out.rearrange("(t p) d -> p t d", p=128)

        def finished(i, a):
            if i % 4 == 3:
                sp.dma(l_o, ov[:, i - 3:i + 1, :], X[:, i - 3:i + 1, :], a)

        def attention(t_x, t_x2):
            area = Area(0)
            HFh, HFl = area.pair(2, 2048)
            QK = area.ring(2, 16, 256)
            PB = area.ring(3, 2, 16, 64)
            Wq, Wu = area.pair(2, 1024), area.pair(2, 256)
            xnr, vr1 = area.ring(3, D), area.ring(3, 2, 128)
            SM = area.ring(4, 2, 16)
            RS = area.ring(1, 16, 16)
            wst = PB.bufs[0].rearrange('p q k f -> p (q k f)').rearrange('p (a b) -> p a b', a=2)
            wsu = PB.bufs[1].rearrange('p q k f -> p (q k f)')[:, 0:512].rearrange('p (a b) -> p a b', a=2)
            assert area.at <= 4 * 3 * 2048
            PV = area.ring(1, 2, 1024)
            ET = area.ring(2, 16, 16, 16)
            DF = area.ring(2, 2, 16, 16)
            OB = area.ring(2, 16, 64)
            xnr2 = Ring(xnr.bufs + [view(area.at + 256 * n, D) for n in range(4)])
            vr2 = Ring(vr1.bufs + [view(area.at + 256 * n, 2, 128) for n in range(4, 11)])
            OI, OIP, OIT = area.ring(4, D), area.ring(2, 2, D, dt=f16), area.ring(2, 4, 128, dt=f16)
            YG, GS = area.ring(2, D), area.ring(2, D)
            before = now()
            l_w1 = sem("l_w1")
            sp.dma(l_w1, wst, qkvw_in.rearrange("(k p) n -> p k n", p=128), before)
            t_w1 = sp.dma(l_w1, wsu, wout_in.rearrange("(k p) n -> p k n", p=128), before)
            for q in (dve, act, pool, pe):
                q.wait(before)
            flat = "p a b -> p (a b)"
            t_wq = split([w.rearrange(flat) for w in Wq], wst.rearrange(flat), pool, t_w1)
            t_wq += split([w.rearrange(flat) for w in Wu], wsu.rearrange(flat), pool, t_w1)
            OW = dram("OW", [T * 4, 64])
            tr = Ring([ps[6], ps[7]])
            qb = Ring([ps[0], ps[1]])
            sb_ = Ring([ps[2], ps[3], ps[4]])
            eb = Ring([ps[5]])
            l_ow = [sem(f"l_ow{i}") for i in range(8)]

            def place(n, v):
                h0, b = 4 * (n // 4), n % 4

                def at(h_):
                    return h_.rearrange("p k (h b t) -> p k h b t", h=16, b=4)[:, :, h0:h0 + 4, b, :]
                return at(HFh), at(HFl), v.rearrange("p k (h t) -> p k h t", h=4)

            t_read = [None] * 16

            def norms(bh):
                ends = []
                tiles = [16 * bh + 4 * (n % 4) + n // 4 for n in range(16)]
                return ends, norm_T(1, place, ((xnr, vr1), (xnr2, vr2))[bh], tr, lambda i: t_x[i], tiles, ends)

            def project(buf, h, ci, t_h):
                qk, free, t_cp = buf
                bk, bfree, busers = qb.next()
                for k in range(2):
                    m = mm3(bk[:, 0:256], (HFh[:, k, 128 * h:128 * h + 128], HFl[:, k, 128 * h:128 * h + 128]),
                            [w[:, k, 256 * ci:256 * ci + 256] for w in Wq], k == 0, k == 1,
                            t_h, bfree, t_wq, mark=(k == 1))
                a = copy(act, qk[:, h, :], bk[:, 0:256], m, free)
                busers.append(a)
                t_cp.append(a)
                t_read[h] = m

            def scores(qk, t_cp, q2, by=(pool, pool)):
                pb, pfree, pusers = PB.next()
                ms = []
                for q in range(2):
                    ms.append(tt(by[q], pb[:, q], bc(qk[:, 2 * q2 + q, 0:64], 1, 16), qk[:, :, 64:128], ALU.mult,
                                 t_cp, pfree, t_wq))
                bk, bfree, busers = sb_.next()
                pv = pb.rearrange("p q k (f d) -> p (q k f) d", d=4)
                for d in range(4):
                    m = mm(bk[:, :], ident[:, :], pv[:, :, d], d == 0, d == 3, ms, bfree, mark=(d == 3))
                pusers.append(m)
                return bk, m, busers

            def soft(et, efree, q2, bk, m, busers):
                s4 = bk[:, :].rearrange("p (q k f) -> p q k f", q=2, k=16)
                sm, sfree, susers = SM.next()
                df, dfree, dusers = DF.next()
                a = dve(lambda e: e.tensor_reduce(sm, s4.rearrange("p q k f -> p q f k"), AX.X, ALU.max), m, sfree)
                a = tt(dve, df, s4, bc(sm, 2, 16), ALU.subtract, a, dfree)
                busers.append(a)
                susers.append(a)
                a = act(lambda e: e.activation(et[:, :, 2 * q2:2 * q2 + 2, :].rearrange("p k q f -> p q k f"), df,
                                               ACT.Exp, scale=0.5), a, efree)
                dusers.append(a)
                return a

            def values(qk, q2, ob, ofree, et, a, by=(dve, dve)):
                pv, pfree, pusers = PV.next()
                ms = []
                for q in range(2):
                    ms.append(tt(by[q], pv[:, q].rearrange("p (f d k) -> p f d k", f=16, d=4),
                                 bc(et[:, :, 2 * q2 + q, :].rearrange("p k f -> p f k"), 2, 4),
                                 qk[:, :, 128:192].rearrange("p k (f d) -> p f d k", d=4), ALU.mult, a, pfree))
                o2 = ob[:, 2 * q2:2 * q2 + 2, :]
                r = dve(lambda e: e.tensor_reduce(o2, pv.rearrange("p q (n k) -> p (q n) k", k=16), AX.X, ALU.add), ms, ofree)
                pusers.append(r)
                return r, ms

            def totals(et, a):
                bk, bfree, busers = eb.next()
                for k in range(16):
                    m = mm(bk[:, 0:256], ident[:, :], et[:, k].rearrange("p q f -> p (q f)"), k == 0, k == 15,
                           a, bfree, mark=(k == 15))
                return bk, m, busers

            def finish(c, qk, qusers, ob, ousers, r, bk, m, busers):
                bh, ci = c // 4, c % 4
                rs, rfree, rusers = RS.next()
                a = dve(lambda e: e.reciprocal(rs.rearrange("p q f -> p (q f)"), bk[:, 0:256]), m, rfree)
                busers.append(a)
                a = tt(dve, rs4(ob), rs4(ob), bc(rs, 3, 4), ALU.mult, a, r)
                rusers.append(a)
                a = tt(dve, ob, ob, qk[:, :, 192:256], ALU.mult, a)
                qusers.append(a)
                for b in range(4):
                    r0 = (ci * 8 + bh * 4 + b) * 512
                    t_o = sp.dma(l_ow[c], OW[r0:r0 + 512, :].rearrange("(h t) f -> t h f", t=32),
                                 ob[32 * b:32 * b + 32, :, :], a)
                ousers.append(t_o)
                for b in range(4):
                    stored[8 * ci + 4 * bh + b] = t_o

            def rs4(ob):
                return ob.rearrange("p q (f d) -> p q f d", d=4)

            OWv = OW.rearrange("(t p r) f -> t p (r f)", p=128, r=4)
            l_oi = [sem(f"l_oi{i}") for i in range(4)]
            got = {}

            def w_load(i):
                oi, free, users = OI.next()
                got[i] = oi, sp.dma(l_oi[i % 4], oi, OWv[i], stored[i], free), users

            def w_split(i):
                oi, a, users = got[i]
                op_, pfree, pusers = OIP.next()
                s_ = split((op_[:, 0, :], op_[:, 1, :]), oi, pool, a, pfree)
                users.extend(s_)
                got[i] = op_.rearrange("p a b -> p (a b)"), s_, pusers

            def w_turn(i):
                fl, s_, pusers = got[i]
                bk, bfree, busers = tr.next()
                b16 = shaped(bk[:, 0:256].bitcast(f16), (4, 128))
                for k in range(4):
                    m = tp16(b16[:, k, :], fl[:, k * 128:(k + 1) * 128], s_, bfree, mark=(k == 3))
                pusers.append(m)
                got[i] = b16, m, busers

            def w_copy(i):
                b16, m, busers = got[i]
                ot, tfree, tusers = OIT.next()
                a = copy(act, ot, b16, m, tfree)
                busers.append(a)
                got[i] = ot, a, tusers

            def w_product(i):
                if i % 4 == 0:
                    gk, gfree, gusers = qb.next()
                    gs, sfree, susers = GS.next()
                    a = copy(act, gs, gk[:, 0:256], gates(1, 0, gk, i // 4, gfree), sfree)
                    gusers.append(a)
                    got["g"] = gs, susers, a
                ot, a, tusers = got[i]
                bk, bfree, busers = qb.next()
                for k in range(2):
                    m = mm3(bk[:, 0:256], (ot[:, k, :], ot[:, 2 + k, :]), [w[:, k, :] for w in Wu], k == 0, k == 1,
                            a, bfree, mark=(k == 1))
                tusers.append(m)
                got[i] = bk, m, busers, got["g"]

            def w_add(i):
                bk, m, busers, (gs, susers, t_g) = got.pop(i)
                yg, yfree, yusers = YG.next()
                y = tt(dve, yg, bk[:, 0:256], gs, ALU.mult, m, yfree, t_g)
                busers.append(y)
                if i % 4 == 3:
                    susers.append(y)
                y = tt((pool, dve)[i % 2], X[:, i, :], X[:, i, :], yg, ALU.add, y)
                yusers.append(y)
                got[i] = y

            def w_settle(i):
                settled(i, got.pop(i), t_x2, 4)

            w_stages = [w_load, lambda i: None, w_split, w_turn, w_copy, w_product, w_add, w_settle]
            stored = {}
            ends, stages = norms(0)
            bufs = [(*QK.next(), )]
            bufs[0] = (bufs[0][0], bufs[0][1], [], bufs[0][2])
            idle = lambda n: None
            stages += [idle, idle, idle, lambda n: project(bufs[0][:3], n, 0, ends[0:4 * (n // 4) + 4])]
            for t in range(16 + len(stages) - 1):
                yield
                pipeline(16, stages, t, t + 1)
            everything = now()
            for r in (sb_, eb):
                r.free = [list(everything) for _ in r.bufs]
            for q in (dve, act):
                q.wait(everything)
            chunk, sc, sf = {}, {}, {}
            N = 64

            def do_scores(s_):
                if s_ < N:
                    qk, free, t_cp, qusers = bufs[s_ // 8]
                    sc[s_] = scores(qk, t_cp, s_ % 8, ((dve, dve), (dve, pool), (pool, pool))[min(s_, 2)])

            def do_soft(s_):
                if s_ < N:
                    if s_ % 8 == 0:
                        chunk[s_ // 8] = ET.next()
                    et, efree, eusers = chunk[s_ // 8]
                    sf[s_] = soft(et, efree, s_ % 8, *sc.pop(s_))
            do_scores(0)
            do_scores(1)
            do_soft(0)
            pend = None
            for s_ in range(N):
                c, q2 = s_ // 8, s_ % 8
                qk, free, t_cp, qusers = bufs[c]
                et, efree, eusers = chunk[c]
                if q2 == 0:
                    ob, ofree, ousers = OB.next()
                if c == 2 and q2 == 6:
                    lo_by[1] = dve
                    ends2, stages = norms(1)
                    stages[3] = (lambda f: lambda n: (act.wait(t_read[4 * (n // 4):4 * (n // 4) + 4]), f(n)))(stages[3])
                    idle = lambda n: None
                    stages = [stages[0], idle, stages[1], idle, *stages[2:4], idle, idle, idle, stages[4]]

                def tick(n):
                    if 22 <= s_ < 32:
                        pipeline(16, stages, 4 * (s_ - 22) + n, 4 * (s_ - 22) + n + 1)
                if c < 7:
                    if q2 == 1:
                        nq, nfree, nusers = QK.next()
                        bufs.append((nq, nfree, [], nusers))
                    if c == 3:
                        heads = range(4 * (q2 - 2), 4 * (q2 - 2) + 4) if 2 <= q2 < 6 else ()
                    else:
                        heads = range(3 * (q2 - 1), 3 * (q2 - 1) + 3 + (q2 == 5)) if 1 <= q2 < 6 else ()
                do_scores(s_ + 2)
                if c < 7:
                    for h in heads:
                        project(bufs[c + 1][:3], h, (c + 1) % 4, (ends if c < 3 else ends2)[0:4 * (h // 4) + 4])
                tick(0)
                do_soft(s_ + 1)
                tick(1)
                tick(2)
                r, last = values(qk, q2, ob, ofree, et, sf[s_], (dve, pool if s_ >= 61 else dve))
                tick(3)
                if s_ == N - 1:
                    tr, qb = Ring([ps[2]]), Ring([ps[1], ps[3]])
                    for ring in (tr, qb):
                        ring.free = [list(w_free) for _ in ring.bufs]
                w_free = now()
                if q2 == 7:
                    tot = totals(et, [sf[8 * c + n] for n in range(8)])
                    eusers.extend([*last, tot[1]])
                    pend = (c, qk, qusers, ob, ousers, r, *tot)
                if q2 == 0 and pend:
                    finish(*pend)
                    pend = None
            pipeline(NT, w_stages, 0, 6)
            finish(*pend)
            yield True
            for t in range(6, NT + len(w_stages) - 1):
                pipeline(NT, w_stages, t, t + 1)
                yield

        t_x1, t_x2 = [], []
        before = now()
        phase_sems(1)
        beside = attention(t_x1, t_x2)
        moe(0, 4, 2, rw_in, rb_in, True, before, t_x, t_conv, t_x1, beside)
        t_conv = [[(s_, s_.n) for s_ in sv_sem]]
        while next(beside) is None:
            pass
        before = now()
        phase_sems(3)
        moe(1, 8, 1, wr_in, br_in, False, before, t_x2, t_conv, [], None, beside)

        sp.wait((l_o, l_o.n))

        block = ctx.enter_context(nc.Block())
        block.sync(sp.play)
        block.gpsimd(pool.play)
        block.scalar(act.play)
        block.vector(dve.play)
        block.tensor(pe.play)


def lay_out(i, np):
    a = {k: np.ascontiguousarray(v) for k, v in i.items()}
    return {
        "x": a["L0_attn_query"].reshape(T, D),
        "wqk": np.ascontiguousarray(np.concatenate([a["L0_attn_W_Q"][:, :, 0], a["L0_attn_W_K"][:, :, 0]]).T),
        "wv": np.ascontiguousarray(a["L0_attn_W_V"].transpose(1, 0, 2).reshape(D, 1024)),
        "wo": np.ascontiguousarray(a["L0_attn_W_O"].transpose(2, 1, 0).reshape(1024, D)),
        "rw": a["L0_ffn_router_w"], "rb": a["L0_ffn_router_b"],
        "w1": a["L0_ffn_w1"], "w3": a["L0_ffn_w3"], "w2": a["L0_ffn_w2"],
        "c0": a["L0_c"], "m0": a["L0_wmod"],
        "qkvw": a["L1_attn_w_qkvw"], "wout": a["L1_attn_w_out"],
        "wr": a["L1_ffn_Wr"], "br": a["L1_ffn_br"], "v1": a["L1_ffn_W1"], "v2": a["L1_ffn_W2"],
        "c1": a["L1_c"], "m1": a["L1_wmod"],
    }


def kernel(**inputs):
    import numpy as np
    import concourse.bacc as bacc
    from concourse.bass_utils import run_bass_kernel_spmd

    nc = bacc.Bacc("TRN2", target_bir_lowering=False, num_devices=1)
    arrays = {f"in_{k}": v for k, v in lay_out(inputs, np).items()}
    args = [nc.dram_tensor(k, v.shape, mybir.dt.from_np(v.dtype), kind="ExternalInput").ap() for k, v in arrays.items()]
    out = nc.dram_tensor("out_0", (T, D), fp32, kind="ExternalOutput").ap()
    program(nc, *args, out)
    r = run_bass_kernel_spmd(nc, [arrays], core_ids=[0])
    return r.results[0]["out_0"].reshape(B, S, D)
```
